# Optimizing a Trainium2 kernel written in Bass

```python
import numpy as np
import jax
import jax.numpy as jnp

def _softmax(x, axis=-1):
    return jax.nn.softmax(x, axis=axis)

def _gelu(x):
    return jax.nn.gelu(x, approximate=True)

def _silu(x):
    return jax.nn.silu(x)

def _sigmoid(x):
    return jax.nn.sigmoid(x)

def _layernorm(x, axis=-1, eps=1e-05):
    m = jnp.mean(x, axis=axis, keepdims=True)
    v = jnp.var(x, axis=axis, keepdims=True)
    return (x - m) / jnp.sqrt(v + eps)

def _scatter_add(tgt, idx, src, axis=0):
    return tgt.at[idx].add(src)

def _segment_sum(src, seg, n):
    return jax.ops.segment_sum(src, seg, n)
kernel_name = 'mk_flamingo_gated_d1_seqx_r4_2958f5'

def setup_inputs(seed: int=0):
    np.random.seed(seed)
    _w = jnp.asarray

    def _rec_inputs():
        import jax
        import jax.numpy as jnp
        _rk = jax.random.key(seed)
        x = -0.0002928 + 1 * jax.random.normal(jax.random.fold_in(_rk, 1), (16, 256, 256), jnp.float32)
        _lenS = 256 - jax.random.randint(jax.random.fold_in(_rk, 7), (16,), 0, max(1, 256 // 4) + 1, jnp.int32)
        _lenS2 = 256 - jax.random.randint(jax.random.fold_in(_rk, 8), (16,), 0, max(1, 256 // 4) + 1, jnp.int32)
        _ctx_1024P = jax.random.normal(jax.random.fold_in(_rk, 11), (16, 16, 256), jnp.float32)
        _ctx_1024c = jax.random.dirichlet(jax.random.fold_in(_rk, 511), 0.3 * jnp.ones((16,), jnp.float32), (16, 256))
        _ctx_1024t = jnp.einsum('bsk,bkd->bsd', _ctx_1024c, _ctx_1024P)
        _ctx_1024t = _ctx_1024t * jax.lax.rsqrt(jnp.mean(jnp.square(_ctx_1024t)) + 1e-12) * 0.953939
        ctx_1024 = -1.39393e-06 + 0.999914 * (_ctx_1024t + 0.3 * jax.random.normal(jax.random.fold_in(_rk, 611), (16, 256, 256), jnp.float32))
        _g = jax.random.normal(jax.random.fold_in(_rk, 9001), (2, 1), jnp.float32)
        _g = jnp.sign(_g) * jnp.maximum(jnp.abs(_g), 1.0) + (_g == 0) * 1.0
        g_xattn = _g[0]
        g_ffn = _g[1]
        return (x, ctx_1024, g_xattn, g_ffn)
    x, ctx_1024, g_xattn, g_ffn = _rec_inputs()

    def _L0_xattn_setup():
        import jax, jax.numpy as jnp
        import numpy as np
        B, S, D, NH = (2, 512, 256, 8)
        DH = D // NH
        EPS = 1e-06
        LN_EPS = 1e-05

        def _mlstm_cell(q, k, v, igate_w, igate_b, fgate_w, fgate_b, ln_scale):
            Slen = q.shape[0]
            ifg = jnp.concatenate([q, k, v], axis=-1)
            ig = (ifg @ igate_w.T + igate_b).T
            fg = (ifg @ fgate_w.T + fgate_b).T
            qh = q.reshape(Slen, NH, DH).transpose(1, 0, 2)
            kh = k.reshape(Slen, NH, DH).transpose(1, 0, 2)
            vh = v.reshape(Slen, NH, DH).transpose(1, 0, 2)
            log_f = jax.nn.log_sigmoid(fg)
            cs = jnp.cumsum(log_f, axis=1)
            fg_mat = cs[:, :, None] - cs[:, None, :]
            mask = jnp.tril(jnp.ones((Slen, Slen), dtype=bool))
            log_fg_mat = jnp.where(mask, fg_mat, -jnp.inf)
            log_D = log_fg_mat + ig[:, None, :]
            max_log_D = jnp.max(log_D, axis=-1, keepdims=True)
            D_mat = jnp.exp(log_D - max_log_D)
            qk = jnp.einsum('hsd,htd->hst', qh, kh) / np.sqrt(DH)
            C = qk * D_mat
            normalizer = jnp.maximum(jnp.abs(C.sum(axis=-1, keepdims=True)), jnp.exp(-max_log_D))
            h = jnp.einsum('hst,htd->hsd', C / (normalizer + EPS), vh)
            h = h.transpose(1, 0, 2).reshape(Slen, D)
            mu = h.mean(axis=-1, keepdims=True)
            var = h.var(axis=-1, keepdims=True)
            return (h - mu) / jnp.sqrt(var + LN_EPS) * ln_scale
        key = jax.random.key(seed)
        ks = jax.random.split(key, 8)
        rnd = lambda k, sh, s=1.0: jax.random.normal(k, sh, dtype=jnp.float32) * s
        return {'q': rnd(ks[0], (B, S, D)), 'k': rnd(ks[1], (B, S, D)), 'v': rnd(ks[2], (B, S, D)), 'igate_w': rnd(ks[3], (NH, 3 * D), 0.02), 'igate_b': jnp.linspace(3.0, 6.0, NH, dtype=jnp.float32), 'fgate_w': rnd(ks[4], (NH, 3 * D), 0.02), 'fgate_b': rnd(ks[5], (NH,), 0.3162278), 'ln_scale': jnp.ones((D,), dtype=jnp.float32)}
    _L0_xattn_all = _L0_xattn_setup()
    _L0_xattn_in = {k: v for k, v in _L0_xattn_all.items() if k in ('igate_w', 'igate_b', 'fgate_w', 'fgate_b', 'ln_scale')}
    del _L0_xattn_all

    def _L0_ffn_setup():
        import jax, jax.numpy as jnp
        import numpy as np
        EXPERTS = 8
        TOP_K = 2

        def swiglu(x, w1, w2, w3):
            h = x @ w1
            return h * jax.nn.sigmoid(h) * (x @ w2) @ w3
        key = jax.random.key(seed)
        ks = jax.random.split(key, 9)
        B, S, D = (4, 512, 256)
        H = 2 * D
        s = 0.02
        x = jax.random.normal(ks[0], (B, S, D), dtype=jnp.float32)
        gate_w = jax.random.normal(ks[1], (D, EXPERTS), dtype=jnp.float32) * s
        ew1 = jax.random.normal(ks[2], (EXPERTS, D, H), dtype=jnp.float32) * s
        ew2 = jax.random.normal(ks[3], (EXPERTS, D, H), dtype=jnp.float32) * s
        ew3 = jax.random.normal(ks[4], (EXPERTS, H, D), dtype=jnp.float32) * s
        sw1 = jax.random.normal(ks[5], (D, H), dtype=jnp.float32) * s
        sw2 = jax.random.normal(ks[6], (D, H), dtype=jnp.float32) * s
        sw3 = jax.random.normal(ks[7], (H, D), dtype=jnp.float32) * s
        return {'x': x, 'gate_w': gate_w, 'ew1': ew1, 'ew2': ew2, 'ew3': ew3, 'sw1': sw1, 'sw2': sw2, 'sw3': sw3}
    _L0_ffn_all = _L0_ffn_setup()
    _L0_ffn_in = {k: v for k, v in _L0_ffn_all.items() if k in ('gate_w', 'ew1', 'ew2', 'ew3', 'sw1', 'sw2', 'sw3')}
    del _L0_ffn_all
    return {'x': x, 'ctx_1024': ctx_1024, 'g_xattn': g_xattn, 'g_ffn': g_ffn, 'L0_xattn_igate_w': _L0_xattn_in['igate_w'], 'L0_xattn_igate_b': _L0_xattn_in['igate_b'], 'L0_xattn_fgate_w': _L0_xattn_in['fgate_w'], 'L0_xattn_fgate_b': _L0_xattn_in['fgate_b'], 'L0_xattn_ln_scale': _L0_xattn_in['ln_scale'], 'L0_ffn_gate_w': _L0_ffn_in['gate_w'], 'L0_ffn_ew1': _L0_ffn_in['ew1'], 'L0_ffn_ew2': _L0_ffn_in['ew2'], 'L0_ffn_ew3': _L0_ffn_in['ew3'], 'L0_ffn_sw1': _L0_ffn_in['sw1'], 'L0_ffn_sw2': _L0_ffn_in['sw2'], 'L0_ffn_sw3': _L0_ffn_in['sw3']}

def reference(x, ctx_1024, g_xattn, g_ffn, L0_xattn_igate_w, L0_xattn_igate_b, L0_xattn_fgate_w, L0_xattn_fgate_b, L0_xattn_ln_scale, L0_ffn_gate_w, L0_ffn_ew1, L0_ffn_ew2, L0_ffn_ew3, L0_ffn_sw1, L0_ffn_sw2, L0_ffn_sw3):
    import jax
    import jax.numpy as jnp

    def _L0_xattn_ref(q, k, v, igate_w, igate_b, fgate_w, fgate_b, ln_scale):
        import jax, jax.numpy as jnp
        import numpy as np
        B, S, D, NH = (2, 512, 256, 8)
        DH = D // NH
        EPS = 1e-06
        LN_EPS = 1e-05

        def _mlstm_cell(q, k, v, igate_w, igate_b, fgate_w, fgate_b, ln_scale):
            Slen = q.shape[0]
            ifg = jnp.concatenate([q, k, v], axis=-1)
            ig = (ifg @ igate_w.T + igate_b).T
            fg = (ifg @ fgate_w.T + fgate_b).T
            qh = q.reshape(Slen, NH, DH).transpose(1, 0, 2)
            kh = k.reshape(Slen, NH, DH).transpose(1, 0, 2)
            vh = v.reshape(Slen, NH, DH).transpose(1, 0, 2)
            log_f = jax.nn.log_sigmoid(fg)
            cs = jnp.cumsum(log_f, axis=1)
            fg_mat = cs[:, :, None] - cs[:, None, :]
            mask = jnp.tril(jnp.ones((Slen, Slen), dtype=bool))
            log_fg_mat = jnp.where(mask, fg_mat, -jnp.inf)
            log_D = log_fg_mat + ig[:, None, :]
            max_log_D = jnp.max(log_D, axis=-1, keepdims=True)
            D_mat = jnp.exp(log_D - max_log_D)
            qk = jnp.einsum('hsd,htd->hst', qh, kh) / np.sqrt(DH)
            C = qk * D_mat
            normalizer = jnp.maximum(jnp.abs(C.sum(axis=-1, keepdims=True)), jnp.exp(-max_log_D))
            h = jnp.einsum('hst,htd->hsd', C / (normalizer + EPS), vh)
            h = h.transpose(1, 0, 2).reshape(Slen, D)
            mu = h.mean(axis=-1, keepdims=True)
            var = h.var(axis=-1, keepdims=True)
            return (h - mu) / jnp.sqrt(var + LN_EPS) * ln_scale
        return jax.vmap(lambda qq, kk, vv: _mlstm_cell(qq, kk, vv, igate_w, igate_b, fgate_w, fgate_b, ln_scale))(q, k, v)

    def _L0_ffn_ref(x, gate_w, ew1, ew2, ew3, sw1, sw2, sw3):
        import jax, jax.numpy as jnp
        import numpy as np
        EXPERTS = 8
        TOP_K = 2

        def swiglu(x, w1, w2, w3):
            h = x @ w1
            return h * jax.nn.sigmoid(h) * (x @ w2) @ w3
        B, S, D = x.shape
        gate_out = x @ gate_w
        top_v, top_i = jax.lax.top_k(gate_out, TOP_K)
        masked = jnp.full_like(gate_out, -1e+20)
        bi = jnp.arange(B)[:, None, None]
        si = jnp.arange(S)[None, :, None]
        masked = masked.at[bi, si, top_i].set(top_v)
        probs = jax.nn.softmax(masked, axis=-1)
        chosen = jnp.zeros_like(gate_out, dtype=bool).at[bi, si, top_i].set(True)
        w = jnp.where(chosen, probs, 0.0)

        def one_expert(w1, w2, w3, we):
            return swiglu(x, w1, w2, w3) * we[..., None]
        out = jax.vmap(one_expert, in_axes=(0, 0, 0, 2))(ew1, ew2, ew3, w).sum(0)
        out = out + swiglu(x, sw1, sw2, sw3)
        return out
    x = x + jnp.tanh(g_xattn[0]) * _L0_xattn_ref(_layernorm(x, axis=-1), ctx_1024, ctx_1024, L0_xattn_igate_w, L0_xattn_igate_b, L0_xattn_fgate_w, L0_xattn_fgate_b, L0_xattn_ln_scale)
    x = x + jnp.tanh(g_ffn[0]) * _L0_ffn_ref(_layernorm(x, axis=-1), L0_ffn_gate_w, L0_ffn_ew1, L0_ffn_ew2, L0_ffn_ew3, L0_ffn_sw1, L0_ffn_sw2, L0_ffn_sw3)
    return x

_drawn_inputs = setup_inputs


def setup_inputs(seed=0):
    import zlib

    import numpy as np

    out = dict(_drawn_inputs(seed))
    spreads = {'L0_xattn_ln_scale': (1.0, 0.2)}
    factors = {'L0_ffn_gate_w': 5.693,
     'L0_ffn_ew1': 4.998,
     'L0_ffn_ew2': 4.951,
     'L0_ffn_ew3': 4.948,
     'L0_ffn_sw1': 3.569,
     'L0_ffn_sw2': 3.514,
     'L0_ffn_sw3': 3.53}
    for name, (base, spread) in spreads.items():
        noise = np.random.default_rng([zlib.crc32(name.encode()), seed]).standard_normal(out[name].shape)
        drawn = base * np.exp(spread * noise) if base else spread * noise
        out[name] = jnp.asarray(drawn.astype(out[name].dtype))
    for name, factor in factors.items():
        out[name] = (out[name] * factor).astype(out[name].dtype)
    return out
```

```python
from contextlib import ExitStack

import concourse.bass as bass
from concourse import mybir

F32 = mybir.dt.float32
F16 = mybir.dt.float16
BF16 = mybir.dt.bfloat16
I32 = mybir.dt.int32
U32 = mybir.dt.uint32
ALU = mybir.AluOpType
ACT = mybir.ActivationFunctionType
AX = mybir.AxisListType

P = 128
LN_EPS = 1e-5
DEN_EPS = 1e-6
MASKED = -1e30


def at(n, count=1):
    return bass.ds(n, count)


def wait_from(eng, sem, value):
    if isinstance(value, int) and value <= 0:
        return
    eng.wait_ge(sem, value)


class Steps:

    def __init__(self, eng, sem, base=0):
        self.eng, self.sem, self.base, self.n = eng, sem, base, 0

    def then(self, instruction):
        instruction.then_inc(self.sem, 1)
        self.n += 1
        self.eng.wait_ge(self.sem, self.base + self.n)


def stepped(eng, unroll, total, step):
    for u in range(unroll):
        step(u, u, 0)
    with eng.Fori(1, total // unroll) as i:
        for u in range(unroll):
            step(unroll * i + u, u, i)


def looped(eng, unroll, first, end, step):
    with eng.Fori(0, (end - first) // unroll) as i:
        for u in range(unroll):
            step(unroll * i + (first + u), (first + u) % unroll, i + (first + u) // unroll)


def flamingo_block(nc, x, ctx_in, g_xattn, g_ffn, igate_w, igate_b, fgate_w, fgate_b, ln_scale,
                   gate_w, ew1, ew2, ew3, sw1, sw2, sw3, out):
    B, S, D = x.shape
    NH = igate_w.shape[0]
    DH = D // NH
    E = gate_w.shape[1]
    HID = ew1.shape[2]
    TPB = S // P
    TT = B * TPB
    C = D // P
    HPC = NH // C
    BH = B * NH
    assert BH == P and DH == 32 and HID == 4 * P and TPB == 2
    QK_SCALE = DH ** -0.5
    KH = HID // P
    PIECE = C * HID
    PIECES = 3 * (E + 1)
    TOP = 2
    NT = (TOP * TT * P + E * (P - 1)) // P
    ROW = 2 * D + 32

    es = ExitStack()
    with es:
        def sb(name, shape, dt, stack=es):
            return stack.enter_context(nc.sbuf_tensor(name, shape, dt))

        def sem(name):
            return es.enter_context(nc.semaphore(name))

        x_v = x.rearrange("b (t p) d -> p (b t) d", p=P)
        c_v = ctx_in.rearrange("b (t p) d -> p (b t) d", p=P)
        out_v = out[0:TT * P, :].rearrange("(t p) d -> p t d", p=P)
        qk = nc.dram_tensor("qk_split", [B, 2, 2, NH, DH, S], F16, kind="Internal").ap()
        slots = nc.dram_tensor("slots", [NT * P, ROW // 2], U32, kind="Internal").ap()
        am = nc.dram_tensor("gate_parts", [3, 2, BH, S], BF16, kind="Internal").ap()

        ident = sb("ident", [P, P], F32)
        ident_h = sb("ident_h", [P, P], F16)
        earlier = sb("earlier", [P, P], BF16)
        ones_b = sb("ones_b", [P, P], BF16)
        pad_row = sb("pad_row", [P, ROW // 2], U32)
        xs = sb("xs", [P, TT, D], F32)
        half = sb("half", [P, TT], F32)
        small = sb("small", [P, 8, TT], F32)
        mean = sb("mean", [P, TT], F32)
        rstd = sb("rstd", [P, TT], F32)
        stats = sb("stats", [P, TT, 6], F32)
        gains = sb("gains", [P, 2], F32)
        gains_in = sb("gains_in", [P, 2], F32)
        ps = es.enter_context(nc.psum_tensor("ps", [P, 8, 512], F32))

        early = ExitStack()
        with early:
            ln_gain = sb("ln_gain", [P, D], F32, early)
            ident_b = sb("ident_b", [P, P], BF16, early)
            causal = sb("causal", [P, P], BF16, early)
            v_ext = sb("v_ext", [P, TT, NH, DH + 1], F32, early)
            gw_rows = sb("gw_rows", [2 * NH, 3 * D], F32, early)
            gw_sum = sb("gw_sum", [P, 2, C, 2 * NH], F32, early)
            gw = sb("gw", [P, 2, 2, C, 2 * NH], F16, early)
            gw_tmp = sb("gw_tmp", [P, C, 2 * NH], F32, early)
            c_raw = sb("c_raw", [P, 4, TPB, D], F32, early)
            qn = sb("qn", [P, 2, TPB, D], F32, early)
            split = sb("split", [P, 2, 2, 2, C, S], F16, early)
            g_tok = sb("g_tok", [P, TPB, 2, BH], F32, early)
            bias = sb("bias", [P, 2], F32, early)
            ones = sb("ones", [P, S], F32, early)
            zf = sb("zf", [P, S], F32, early)
            zt = sb("zt", [P, S], F32, early)
            lf = sb("lf", [P, S], F32, early)
            cs = sb("cs", [P, S], F32, early)
            am32 = sb("am32", [P, 2, S], F32, early)
            am_r = sb("am_r", [P, 2, S], F32, early)
            am_p = sb("am_p", [P, 3, 2, S], BF16, early)
            nd = sb("nd", [P, S], F32, early)
            en_h = sb("en_h", [P, S], F32, early)
            en = sb("en", [P, TPB, BH], F32, early)
            ks = sb("ks", [3 * DH, 2, NH, S], F16, early)
            qs = sb("qs", [3 * DH, 2, NH, S], F16, early)
            a_rows = sb("a_rows", [6, 2, NH, S], BF16, early)
            m_rows = sb("m_rows", [6, 2, NH, S], BF16, early)
            decay = sb("decay", [P, 2, 2, 3 * P], F32, early)
            cmat = sb("cmat", [P, 2, 2, 3 * P], F32, early)
            den = sb("den", [P, 2, TPB, NH], F32, early)
            hbuf = sb("hbuf", [P, TT, D], F32, early)

        w16 = sb("w16", [P, PIECES, 2, PIECE], F16)
        xr_w = sb("xr", [P, TT, ROW // 2], U32)
        xr = xr_w[:].bitcast(F16)
        stage = sb("stage", [P, 2, PIECE], F32)
        xt = sb("xt", [P, 2, 2 * D], F16)
        slot_i = sb("slot_i", [P, TOP, TT], U32)
        tile_e = sb("tile_e", [P, NT], I32)
        routing = ExitStack()
        with routing:
            xn = sb("xn", [P, 2, D], F32, routing)
            rg = sb("rg", [P, C, E], F32, routing)
            rg16 = sb("rg16", [P, 2, C, E], F16, routing)
            lg = sb("lg", [P, TT, E], F32, routing)
            hot = sb("hot", [P, TOP, TT, E], F32, routing)
            hot_b = sb("hot_b", [P, TT, E], BF16, routing)
            tmp = sb("tmp", [P, TT, E], F32, routing)
            pos = sb("pos", [P, TT, E], F32, routing)
            cum = sb("cum", [P, TT, E], F32, routing)
            top = sb("top", [P, 8, TT], F32, routing)
            slot_f = sb("slot_f", [P, TOP, TT], F32, routing)
            per_e = sb("per_e", [P, 4, E], F32, routing)
            fill = sb("fill", [P, E, TT], F32, routing)
            past = sb("past", [P, NT, E], F32, routing)
            tile_f = sb("tile_f", [P, NT], F32, routing)
            count_i = sb("count_i", [P, NT], I32, routing)
            count_f = sb("count_f", [P, NT], F32, routing)
            rev = sb("rev", [P, E], F32, routing)
            thresh = sb("thresh", [P, TT], F32, routing)
            ones_t = sb("ones_t", [P, TT], F32, routing)
        rows_w = sb("rows", [P, 4, ROW // 2], U32)
        rows = rows_w[:].bitcast(F16)
        act_g = sb("act_g", [P, 2, HID], F32)
        hid = sb("hid", [P, 2, HID], F32)
        hid_t = sb("hid_t", [P, 2, 2, HID], F16)
        y = sb("y", [P, 2, D], F32)
        meta = xr_w[:, :, D:ROW // 2].bitcast(F32)

        gates_ps = ps[:, 4, :].rearrange("p (t g n) -> p t g n", t=TPB, g=2)

        x_in = [sem(f"x_in{u}") for u in range(4)]
        c_in = [sem(f"c_in{u}") for u in range(4)]
        gw_in, vec_in = sem("gw_in"), sem("vec_in")
        consts, pool_step, half_set = sem("consts"), sem("pool_step"), sem("half_set")
        gw_tr, gw_ready = sem("gw_tr"), sem("gw_ready")
        var_ready, rstd_ready = sem("var_ready"), sem("rstd_ready")
        qn_ready, q_tr, k_tr, hi_ready, lo_ready = (sem(n) for n in ("qn_ready", "q_tr", "k_tr", "hi_ready", "lo_ready"))
        split_out = [sem(f"split_out{u}") for u in range(2)]
        gates_done, v_ready = sem("gates_done"), sem("v_ready")
        g_copied, g_tr, exp_ready, ln_ready, nabs_ready = (sem(n) for n in ("g_copied", "g_tr", "exp_ready", "ln_ready", "nabs_ready"))
        nd_ready, en_ready, en_tr, en_tok = (sem(n) for n in ("nd_ready", "en_ready", "en_tr", "en_tok"))
        am_ready, am_out = sem("am_ready"), sem("am_out")
        dve_a, dve_b, dve_c, dve_d = (sem(f"dve_{n}") for n in "abcd")
        heads_in = [sem(f"heads_in{u}") for u in range(2)]
        arg_ready, s_ready, decay_ready, c_ready, h_ready, h_read = (
            sem(n) for n in ("arg_ready", "s_ready", "decay_ready", "c_ready", "h_ready", "h_read"))
        h_stats = sem("h_stats")
        tanh_ready = sem("tanh_ready")
        pad_set, pad_out = sem("pad_set"), sem("pad_out")
        rg_in, rg_ready, numbers, floats = sem("rg_in"), sem("rg_ready"), sem("numbers"), sem("floats")
        xn_ready, xhi_ready, xlo_ready, row_tr, row_copied, logits_done = (
            sem(n) for n in ("xn_ready", "xhi_ready", "xlo_ready", "row_tr", "row_copied", "logits_done"))
        lg_read, gap_ready, gap_exp, hot_ready, ranks_done = (
            sem(n) for n in ("lg_read", "gap_ready", "gap_exp", "hot_ready", "ranks_done"))
        dve_e, routed, meta_set, scattered = sem("dve_e"), sem("routed"), sem("meta_set"), sem("scattered")
        stage_in = [sem(f"stage_in{u}") for u in range(2)]
        rows_in = [sem(f"rows_in{u}") for u in range(4)]
        piece_hi, piece_lo = sem("piece_hi"), sem("piece_lo")
        x_tr, xt_ready, up1, up2, silu, hid_ready, hid_tr, hid_hi, hid_lo, down_done = (
            sem(n) for n in ("x_tr", "xt_ready", "up1", "up2", "silu", "hid_ready", "hid_tr", "hid_hi", "hid_lo",
                             "down_done"))
        y_ready, y_out = sem("y_ready"), [sem(f"y_out{u}") for u in range(2)]
        ye_ready, add_turn, added = sem("ye_ready"), sem("add_turn"), sem("added")

        block = es.enter_context(nc.Block())

        @block.sync
        def _(sp):
            def load_x(b, u, i):
                wait_from(sp, x_in[u], 16 * i)
                sp.dma_start(xs[:, at(TPB * b, TPB)], x_v[:, at(TPB * b, TPB)]).then_inc(x_in[u], 16)

            def load_ctx(b, u, i):
                wait_from(sp, k_tr, b - 3)
                wait_from(sp, v_ready, b - 3)
                sp.dma_start(c_raw[:, u], c_v[:, at(TPB * b, TPB)]).then_inc(c_in[u], 16)

            stepped(sp, 4, B, load_x)
            stepped(sp, 4, B, load_ctx)

            sp.wait_ge(am_out, 16)
            sp.wait_ge(split_out[0], 16 * (B // 2))
            sp.wait_ge(split_out[1], 16 * (B // 2))

            def load_heads(b, u, i):
                wait_from(sp, h_ready, NH // 2 * (b - 1))
                for dst, which, parts in ((qs, 0, (0, 1, 0)), (ks, 1, (0, 0, 1))):
                    for r, part in enumerate(parts):
                        sp.dma_start(dst[DH * r:DH * (r + 1), u],
                                     qk[at(b), which, part].rearrange("o h d s -> d (o h) s")).then_inc(heads_in[u], 16)
                sp.dma_start(m_rows[0:3, u], am[:, 0, at(NH * b, NH), :]).then_inc(heads_in[u], 16)
                sp.dma_start(a_rows[3:6, u], am[:, 1, at(NH * b, NH), :]).then_inc(heads_in[u], 16)

            stepped(sp, 2, B, load_heads)

            def load_piece(src, slot):
                sp.dma_start(stage[:, slot], src).then_inc(stage_in[slot], 16)

            def expert_piece(e, m):
                w, chunks = ((ew1, C), (ew2, C), (ew3, KH))[m]
                return w[at(e)].rearrange("e (c p) n -> p (e c) n", c=chunks)

            sp.wait_ge(h_ready, NH // 2 * B)
            sp.wait_ge(dve_d, 3 * TT)
            for k, w in enumerate((sw1, sw2, sw3)):
                wait_from(sp, piece_lo, k - 1)
                load_piece(w.rearrange("(c p) n -> p c n", p=P), k % 2)
            for k in (3, 4):
                sp.wait_ge(piece_lo, k - 1)
                load_piece(expert_piece(0, k - 3), k % 2)

            def store_shared(n, p):
                sp.wait_ge(y_ready, n + 1)
                sp.dma_start(out_v[:, at(n)], y[:, p:p + 1]).then_inc(y_out[p], 16)

            def shared_turn(n, u, e, m):
                store_shared(n - 1, (u - 1) % 2)
                sp.wait_ge(piece_lo, n + 3)
                load_piece(expert_piece(e, m), u % 2)

            with sp.Fori(0, 3) as i:
                for u in range(6):
                    shared_turn(6 * i + (u + 1), u + 1, 2 * i + (u + 2) // 3, (u + 2) % 3)
            for n in range(19, PIECES - 4):
                shared_turn(n, n, (n + 1) // 3, (n + 1) % 3)
            for n in range(PIECES - 4, TT - 1):
                store_shared(n - 1, (n - 1) % 2)

            sp.wait_ge(scattered, 16 * TOP * TT)

            def load_rows(k, u, i):
                wait_from(sp, added, 16 * (k - 3))
                sp.dma_start(rows_w[:, u], slots[at(P * k, P), :]).then_inc(rows_in[u], 16)

            for k in range(4):
                load_rows(k, k, 0)
            for n in (TT - 2, TT - 1):
                store_shared(n, n % 2)
            looped(sp, 4, 4, NT - 3, load_rows)
            for k in range(NT - 3, NT):
                load_rows(k, k % 4, k // 4)
            sp.wait_ge(added, 16 * NT)

        @block.gpsimd
        def _(pool):
            order = Steps(pool, pool_step)
            pool.dma_start(gw_rows[0:NH, :], igate_w).then_inc(gw_in, 16)
            pool.dma_start(gw_rows[NH:2 * NH, :], fgate_w).then_inc(gw_in, 16)
            pool.dma_start(gains_in[:, 0:1], g_xattn.unsqueeze(0).partition_broadcast(P)).then_inc(vec_in, 16)
            pool.dma_start(gains_in[:, 1:2], g_ffn.unsqueeze(0).partition_broadcast(P)).then_inc(vec_in, 16)
            pool.dma_start(ln_gain[:], ln_scale.unsqueeze(0).partition_broadcast(P)).then_inc(vec_in, 16)
            for b in range(B):
                pool.dma_start(bias[NH * b:NH * (b + 1), 0:1], igate_b.unsqueeze(1)).then_inc(vec_in, 16)
                pool.dma_start(bias[NH * b:NH * (b + 1), 1:2], fgate_b.unsqueeze(1)).then_inc(vec_in, 16)
            order.then(nc.gpsimd.memset(ident[:], 0.0))
            order.then(nc.gpsimd.affine_select(out=ident[:], in_=ident[:], compare_op=ALU.not_equal, fill=1.0,
                                               base=0, pattern=[[-1, P]], channel_multiplier=1))
            nc.gpsimd.tensor_copy(ident_h[:], ident[:])
            order.then(nc.gpsimd.memset(causal[:], 0.0))
            order.then(nc.gpsimd.affine_select(out=causal[:], in_=causal[:], compare_op=ALU.is_ge, fill=MASKED,
                                               base=0, pattern=[[1, P]], channel_multiplier=-1))
            nc.gpsimd.memset(ones[:], 1.0)
            nc.gpsimd.tensor_copy(ident_b[:], ident[:]).then_inc(consts, 1)
            order.then(nc.gpsimd.memset(earlier[:], 1.0))
            order.then(nc.gpsimd.affine_select(out=earlier[:], in_=earlier[:], compare_op=ALU.is_ge, fill=0.0,
                                               base=-1, pattern=[[1, P]], channel_multiplier=-1))
            nc.gpsimd.memset(ones_b[:], 1.0)
            order.then(nc.gpsimd.memset(pad_row[:], 0))
            nc.gpsimd.iota(pad_row[:, D + E:D + E + 1].bitcast(I32), pattern=[[0, 1]], base=TT * P,
                           channel_multiplier=1).then_inc(pad_set, 1)
            pool.wait_ge(pad_set, 1)
            pool.dma_start(slots.rearrange("(t p) r -> p t r", p=P),
                           pad_row[:].unsqueeze(1).broadcast_to([P, NT, ROW // 2])).then_inc(pad_out, 16)
            pool.dma_start(out[TT * P:TT * P + P, :], pad_row[:, 0:D].bitcast(F32)).then_inc(pad_out, 16)
            nc.gpsimd.memset(half[:], -0.5).then_inc(half_set, 1)
            pool.wait_ge(half_set, 1)
            nc.gpsimd.memset(a_rows[:], 1.0)
            nc.gpsimd.memset(m_rows[:], 1.0)
            nc.gpsimd.memset(v_ext[:, :, :, DH:DH + 1], 1.0).then_inc(consts, 1)

            def reciprocal_root(n):
                pool.wait_ge(var_ready, n)
                nc.gpsimd.tensor_tensor(rstd[:], small[:, 6], half[:], ALU.pow).then_inc(rstd_ready, 1)

            reciprocal_root(1)

            def values(b, u, i):
                pool.wait_ge(c_in[u], 16 * i + 16)
                nc.gpsimd.tensor_copy(v_ext[:, at(TPB * b, TPB), :, 0:DH],
                                      c_raw[:, u].rearrange("p t (h d) -> p t h d", h=NH)).then_inc(v_ready, 1)

            stepped(pool, 4, B, values)
            pool.wait_ge(am_ready, 1)
            pool.dma_start(am.rearrange("a k n s -> n a k s"), am_p[:]).then_inc(am_out, 16)
            reciprocal_root(2)
            pool.wait_ge(h_ready, NH // 2 * B)
            pool.wait_ge(dve_d, 3 * TT)
            for c in range(C):
                pool.dma_start(rg[:, c], gate_w[P * c:P * (c + 1), :]).then_inc(rg_in, 16)

            def number(dst, columns, pattern, base):
                order.then(nc.gpsimd.iota(count_i[:, 0:columns], pattern=pattern, base=base, channel_multiplier=0))
                order.then(nc.gpsimd.tensor_copy(dst, count_i[:, 0:columns]))

            number(rev[:], E, [[-1, E]], E)
            number(thresh[:], TT, [[P, TT]], 0)
            number(count_f[:], NT, [[1, NT]], 0)
            nc.gpsimd.memset(ones_t[:], 1.0).then_inc(numbers, 1)
            reciprocal_root(3)
            order.then(nc.gpsimd.memset(meta, 0.0))
            nc.gpsimd.iota(xr_w[:, :, D + E:D + E + 1].bitcast(I32), pattern=[[P, TT], [0, 1]], base=0,
                           channel_multiplier=1).then_inc(meta_set, 1)

            pool.wait_ge(routed, 1)
            pool.wait_ge(meta_set, 2)
            pool.wait_ge(pad_out, 32)
            for k in range(TOP):
                for t in range(TT):
                    nc.gpsimd.indirect_dma_start(
                        out=slots, out_offset=bass.IndirectOffsetOnAxis(ap=slot_i[:, k, t:t + 1], axis=0),
                        in_=xr_w[:, t, :], in_offset=None).then_inc(scattered, 16)

            for p in range(2):
                pool.wait_ge(y_out[p], 16 * TT // 2)

            def add_rows(k, u, i):
                pool.wait_ge(ye_ready, k + 1)
                wait_from(pool, added, 16 * k)
                pool.sem_inc(add_turn, 1)
                nc.gpsimd.indirect_dma_start(
                    out=out, out_offset=bass.IndirectOffsetOnAxis(
                        ap=rows_w[:, u, D + E:D + E + 1], axis=0),
                    in_=y[:, u % 2], in_offset=None, compute_op=ALU.add).then_inc(added, 16)

            for k in range(4):
                add_rows(k, k, 0)
            looped(pool, 4, 4, NT - 3, add_rows)
            for k in range(NT - 3, NT):
                add_rows(k, k % 4, k // 4)

        @block.scalar
        def _(act):
            act.wait_ge(vec_in, 16 * (3 + 2 * B))
            nc.scalar.activation(gains[:], gains_in[:], ACT.Tanh).then_inc(tanh_ready, 1)

            def store_split(b, p):
                act.wait_ge(lo_ready, 2 * b + 2)
                act.dma_start(qk[at(b)].rearrange("o w l (c g) d s -> (g d) (o w l) c s", c=C),
                              split[:, p].rearrange("p w l c s -> p (w l) c s")).then_inc(split_out[p], 16)

            def high(b, u, i):
                p = u % 2
                wait_from(act, split_out[p], 32 * i + 16 * (u // 2))
                wait_from(act, gates_done, b - 1)
                act.wait_ge(q_tr, b + 1)
                nc.scalar.activation(split[:, p, 0, 0], ps[:, p], ACT.Copy).then_inc(hi_ready, 1)
                act.wait_ge(k_tr, b + 1)
                nc.scalar.activation(split[:, p, 1, 0], ps[:, 2 + p], ACT.Copy).then_inc(hi_ready, 1)
                if not isinstance(b, int) or b > 0:
                    store_split(b - 1, 1 - p)

            stepped(act, 4, B, high)
            store_split(B - 1, (B - 1) % 2)

            act.wait_ge(nabs_ready, 1)
            nc.scalar.activation(zt[:], zt[:], ACT.Exp).then_inc(exp_ready, 1)
            act.wait_ge(exp_ready, 1)
            nc.scalar.activation(zt[:], zt[:], ACT.Ln, bias=1.0).then_inc(ln_ready, 1)
            act.wait_ge(nd_ready, 1)
            nc.scalar.activation(en_h[:], nd[:], ACT.Exp, scale=-1.0).then_inc(en_ready, 1)

            def decays(b, u, i):
                for pair in range(NH // 2):
                    n = NH // 2 * b + pair
                    q = pair % 2
                    act.wait_ge(arg_ready, n + 1)
                    wait_from(act, c_ready, n - 1)
                    nc.scalar.activation(decay[:, q], ps[:, 2 * q:2 * q + 2, 0:3 * P], ACT.Exp).then_inc(decay_ready, 1)

            stepped(act, 2, B, decays)

            def piece_high(k, slot, turn):
                act.wait_ge(stage_in[slot], 16 * turn + 16)
                nc.scalar.activation(w16[:, at(k), 0].rearrange("p o n -> p (o n)"), stage[:, slot],
                                     ACT.Copy).then_inc(piece_hi, 1)

            for k in range(3):
                piece_high(k, k % 2, k // 2)

            def copy_rows(n, p):
                act.wait_ge(row_tr, n + 1)
                wait_from(act, logits_done, n - 1)
                nc.scalar.activation(xt[:, p], ps[:, p, 0:D].bitcast(F16), ACT.Copy).then_inc(row_copied, 1)

            def row_high(n, p, i):
                act.wait_ge(xn_ready, n + 1)
                nc.scalar.activation(xr[:, at(n), 0:D].rearrange("p o d -> p (o d)"), xn[:, p], ACT.Copy).then_inc(xhi_ready, 1)
                if not isinstance(n, int) or n > 0:
                    copy_rows(n - 1, 1 - p)

            stepped(act, 2, TT, row_high)
            copy_rows(TT - 1, (TT - 1) % 2)
            act.wait_ge(gap_ready, 1)
            nc.scalar.activation(top[:, 4], top[:, 3], ACT.Exp).then_inc(gap_exp, 1)

            def copy_x(n, p):
                act.wait_ge(x_tr, n + 1)
                wait_from(act, up2, n - 1)
                nc.scalar.activation(xt[:, p], ps[:, 7, 0:D].bitcast(F16), ACT.Copy).then_inc(xt_ready, 1)

            def gate_silu(n, p):
                act.wait_ge(up1, n + 1)
                wait_from(act, hid_ready, n - 1)
                nc.scalar.activation(act_g[:, p], ps[:, p], ACT.Silu).then_inc(silu, 1)

            def hid_high(n, p):
                act.wait_ge(hid_tr, n + 1)
                wait_from(act, down_done, n - 1)
                nc.scalar.activation(hid_t[:, p, 0], ps[:, 4], ACT.Copy).then_inc(hid_hi, 1)

            def expert_y(k, u, i):
                e = act.value_load(tile_e[0:1, at(k)], min_val=0, max_val=E - 1)
                act.wait_ge(down_done, TT + k + 1)
                act.wait_ge(rows_in[u], 16 * i + 16)
                if isinstance(k, int) and k < 2:
                    act.wait_ge(y_out[k], 16 * (TT // 2))
                wait_from(act, added, 16 * (k - 1))
                nc.scalar.activation(y[:, u % 2], ps[:, 5, 0:D], ACT.Copy,
                                     scale=rows_w[:, u, D:D + E].bitcast(F32)[:, at(e)]).then_inc(ye_ready, 1)

            def shared_step(n, p, half, with_piece=True):
                gate_silu(n, p)
                copy_x(n + 1, 1 - p)
                hid_high(n, p)
                if with_piece:
                    piece_high(n + 2, p, half + 1)

            copy_x(0, 0)
            shared_step(0, 0, 0, False)
            shared_step(1, 1, 0)
            shared_step(2, 0, 1)
            looped(act, 2, 3, PIECES - 2, shared_step)
            looped(act, 2, PIECES - 2, TT - 1, lambda n, p, half: shared_step(n, p, half, False))
            shared_step(TT - 1, 1, 0, False)

            def expert_step(k, u, i, last=False):
                gate_silu(TT + k, u % 2)
                if not last:
                    copy_x(TT + k + 1, 1 - u % 2)
                if not isinstance(k, int) or k > 0:
                    expert_y(k - 1, (u - 1) % 4, i if u else i - 1)
                hid_high(TT + k, u % 2)

            for k in range(4):
                expert_step(k, k, 0)
            looped(act, 4, 4, NT - 3, expert_step)
            for k in range(NT - 3, NT):
                expert_step(k, k % 4, k // 4, k == NT - 1)
            expert_y(NT - 1, (NT - 1) % 4, (NT - 1) // 4)

        @block.vector
        def _(dve):
            order = Steps(dve, dve_a)
            dve.wait_ge(gw_tr, 1)
            wt = ps[:, 5, 0:6 * 2 * NH].rearrange("p (k n) -> p k n", k=6)
            nc.vector.tensor_copy(gw_sum[:, 0], wt[:, 0:2])
            order.then(nc.vector.tensor_copy(gw_tmp[:], wt[:, 2:4]))
            order.then(nc.vector.tensor_tensor(gw_sum[:, 1], gw_tmp[:], wt[:, 4:6], ALU.add))
            order.then(nc.vector.tensor_copy(gw[:, :, 0], gw_sum[:]))
            nc.vector.tensor_tensor(gw[:, :, 1], gw_sum[:], gw[:, :, 0], ALU.subtract).then_inc(gw_ready, 1)

            def layer_stats(n):
                me, mo, ve, vo = (stats[:, :, k] for k in (1, 4, 2, 5))
                nc.vector.tensor_tensor(small[:, 0], me, mo, ALU.add)
                nc.vector.tensor_tensor(small[:, 1], me, mo, ALU.subtract)
                order.then(nc.vector.tensor_tensor(small[:, 2], ve, vo, ALU.add))
                nc.vector.tensor_scalar(mean[:], small[:, 0], 0.5, None, ALU.mult)
                order.then(nc.vector.scalar_tensor_tensor(small[:, 3], small[:, 1], 0.25, small[:, 1], ALU.mult, ALU.mult))
                order.then(nc.vector.scalar_tensor_tensor(small[:, 4], small[:, 2], 1.0 / D, small[:, 3], ALU.mult, ALU.add))
                nc.vector.tensor_scalar(small[:, 6], small[:, 4], LN_EPS, None, ALU.add).then_inc(var_ready, 1)
                dve.wait_ge(rstd_ready, n)

            def x_stats(b, u, i):
                dve.wait_ge(x_in[u], 16 * i + 16)
                for t in range(TPB):
                    nc.vector.bn_stats(stats[:, at(TPB * b + t)], xs[:, at(TPB * b + t)])

            stepped(dve, 4, B, x_stats)
            order.then(nc.vector.memset(small[:, 7], 0.0))
            layer_stats(1)

            def queries(b, u, i):
                p = u % 2
                wait_from(dve, q_tr, b - 1)
                for t in range(TPB):
                    n = TPB * b + t
                    last = nc.vector.tensor_scalar(qn[:, p, t], xs[:, at(n)].rearrange("p o d -> p (o d)"),
                                                   mean[:, at(n)], rstd[:, at(n)], ALU.subtract, ALU.mult)
                last.then_inc(qn_ready, 1)

            def low(b, u, i):
                p = u % 2
                for w in range(2):
                    dve.wait_ge(hi_ready, 2 * b + w + 1)
                    nc.vector.tensor_tensor(split[:, p, w, 1].rearrange("p c s -> p (c s)"), ps[:, 2 * w + p],
                                            split[:, p, w, 0].rearrange("p c s -> p (c s)"),
                                            ALU.subtract).then_inc(lo_ready, 1)

            def queries_and_low(b, u, i):
                queries(b, u, i)
                low(b, u, i)

            stepped(dve, 4, B, queries_and_low)

            dve.wait_ge(gates_done, B)
            nc.vector.tensor_copy(g_tok[:].rearrange("p t g n -> p (t g n)"), ps[:, 4]).then_inc(g_copied, 1)
            dve.wait_ge(g_tr, 1)
            dve.wait_ge(vec_in, 16 * (3 + 2 * B))
            ig, fg = ps[:, 5, 0:S], ps[:, 5, S:2 * S]
            order.then(nc.vector.tensor_scalar(zf[:], fg, bias[:, 1:2], None, ALU.add))
            order.then(nc.vector.scalar_tensor_tensor(zt[:], zf[:], -1.0, zf[:], ALU.mult, ALU.min))
            nc.vector.tensor_scalar(zf[:], zf[:], 0.0, None, ALU.min).then_inc(nabs_ready, 1)
            dve.wait_ge(ln_ready, 1)
            order.then(nc.vector.tensor_tensor(lf[:], zf[:], zt[:], ALU.subtract))
            order.then(nc.vector.tensor_tensor_scan(cs[:], ones[:], lf[:], 0.0, ALU.mult, ALU.add))
            order.then(nc.vector.scalar_tensor_tensor(am32[:, 1], ig, bias[:, 0:1], cs[:], ALU.add, ALU.subtract))
            order.then(nc.vector.tensor_tensor_scan(lf[:], am32[:, 1], am32[:, 1], -3e38, ALU.max, ALU.max))
            nc.vector.tensor_tensor(nd[:], cs[:], lf[:], ALU.add).then_inc(nd_ready, 1)
            order.then(nc.vector.tensor_scalar(am32[:, 0], lf[:], -1.0, None, ALU.mult))
            order.then(nc.vector.tensor_copy(am_p[:, 0], am32[:]))
            order.then(nc.vector.tensor_tensor(am_r[:], am32[:], am_p[:, 0], ALU.subtract))
            order.then(nc.vector.tensor_copy(am_p[:, 1], am_r[:]))
            order.then(nc.vector.tensor_tensor(am32[:], am_r[:], am_p[:, 1], ALU.subtract))
            nc.vector.tensor_copy(am_p[:, 2], am32[:]).then_inc(am_ready, 1)
            dve.wait_ge(en_tr, 1)
            nc.vector.tensor_copy(en[:].rearrange("p t n -> p (t n)"), ps[:, 6, 0:S]).then_inc(en_tok, 1)
            dve.wait_ge(en_tok, 1)

            def mix(b, u, i):
                chain = Steps(dve, dve_c, 4 * b)
                for pair in range(NH // 2):
                    n = NH // 2 * b + pair
                    q = pair % 2
                    dve.wait_ge(decay_ready, n + 1)
                    dve.wait_ge(s_ready, n + 1)
                    wait_from(dve, h_ready, n - 1)
                    nc.vector.scalar_tensor_tensor(cmat[:, q], ps[:, 4:6, 0:3 * P], QK_SCALE, decay[:, q],
                                                   ALU.mult, ALU.mult).then_inc(c_ready, 1)
                dve.wait_ge(h_ready, NH // 2 * (b + 1))
                h_ps = ps[:, 6:8, 0:NH * (DH + 1)].rearrange("p t (h e) -> p t h e", h=NH)
                chain.then(nc.vector.scalar_tensor_tensor(den[:, 0], h_ps[:, :, :, DH], -1.0, en[:, :, at(NH * b, NH)],
                                                          ALU.mult, ALU.max))
                chain.then(nc.vector.tensor_tensor(den[:, 1], h_ps[:, :, :, DH], den[:, 0], ALU.max))
                chain.then(nc.vector.tensor_scalar(den[:, 1], den[:, 1], DEN_EPS, None, ALU.add))
                chain.then(nc.vector.reciprocal(den[:, 0], den[:, 1]))
                nc.vector.tensor_tensor(hbuf[:, at(TPB * b, TPB)].rearrange("p t (h d) -> p t h d", h=NH),
                                        h_ps[:, :, :, 0:DH],
                                        den[:, 0].unsqueeze(3).broadcast_to([P, TPB, NH, DH]),
                                        ALU.mult).then_inc(h_read, 1)
                dve.wait_ge(h_read, b + 1)
                for t in range(TPB):
                    last = nc.vector.bn_stats(stats[:, at(TPB * b + t)], hbuf[:, at(TPB * b + t)])
                last.then_inc(h_stats, 1)

            stepped(dve, 2, B, mix)

            dve.wait_ge(h_stats, B)
            layer_stats(2)
            dve.wait_ge(tanh_ready, 1)
            order.then(nc.vector.tensor_scalar(ln_gain[:], ln_gain[:], gains[:, 0:1], None, ALU.mult))

            def residual(n, u, i):
                chain = Steps(dve, dve_d, 3 * n)
                h_n = hbuf[:, at(n)].rearrange("p o d -> p (o d)")
                x_n = xs[:, at(n)].rearrange("p o d -> p (o d)")
                chain.then(nc.vector.scalar_tensor_tensor(h_n, h_n, mean[:, at(n)], ln_gain[:], ALU.subtract, ALU.mult))
                chain.then(nc.vector.scalar_tensor_tensor(x_n, h_n, rstd[:, at(n)], x_n, ALU.mult, ALU.add))
                chain.then(nc.vector.bn_stats(stats[:, at(n)], x_n))

            stepped(dve, 2, TT, residual)
            layer_stats(3)
            dve.wait_ge(rg_in, 16 * C)
            order.then(nc.vector.tensor_copy(rg16[:, 0], rg[:]))
            nc.vector.tensor_tensor(rg16[:, 1], rg[:], rg16[:, 0], ALU.subtract).then_inc(rg_ready, 1)

            def piece_low(k, slot):
                dve.wait_ge(piece_hi, k + 1)
                nc.vector.tensor_tensor(w16[:, at(k), 1].rearrange("p o n -> p (o n)"), stage[:, slot],
                                        w16[:, at(k), 0].rearrange("p o n -> p (o n)"), ALU.subtract).then_inc(piece_lo, 1)

            for k in range(3):
                piece_low(k, k % 2)

            def row_low(n, p):
                dve.wait_ge(xhi_ready, n + 1)
                nc.vector.tensor_tensor(xr[:, at(n), D:2 * D].rearrange("p o d -> p (o d)"), xn[:, p],
                                        xr[:, at(n), 0:D].rearrange("p o d -> p (o d)"), ALU.subtract).then_inc(xlo_ready, 1)

            def normalise(n, p, i):
                wait_from(dve, xlo_ready, n - 1)
                nc.vector.tensor_scalar(xn[:, p], xs[:, at(n)].rearrange("p o d -> p (o d)"), mean[:, at(n)],
                                        rstd[:, at(n)], ALU.subtract, ALU.mult).then_inc(xn_ready, 1)
                if not isinstance(n, int) or n > 0:
                    row_low(n - 1, 1 - p)

            stepped(dve, 2, TT, normalise)
            row_low(TT - 1, (TT - 1) % 2)

            dve.wait_ge(numbers, 1)
            dve.wait_ge(logits_done, TT)
            by_tile = lambda a: a.unsqueeze(2).broadcast_to([P, TT, E])
            by_expert = lambda a: a.unsqueeze(1).broadcast_to([P, TT, E])
            nc.vector.tensor_copy(lg[:].rearrange("p t e -> p (t e)"), ps[:, 6, 0:TT * E]).then_inc(lg_read, 1)
            dve.wait_ge(lg_read, 1)

            def pick(k, values, best):
                order.then(nc.vector.tensor_reduce(top[:, best], values[:], AX.X, ALU.max))
                order.then(nc.vector.tensor_tensor(tmp[:], values[:], by_tile(top[:, best]), ALU.is_equal))
                order.then(nc.vector.tensor_tensor(tmp[:], tmp[:], by_expert(rev[:]), ALU.mult))
                order.then(nc.vector.tensor_reduce(top[:, 2], tmp[:], AX.X, ALU.max))
                order.then(nc.vector.tensor_tensor(hot[:, k], tmp[:], by_tile(top[:, 2]), ALU.is_equal))

            pick(0, lg, 0)
            order.then(nc.vector.scalar_tensor_tensor(lg[:], hot[:, 0], -3e38, lg[:], ALU.mult, ALU.add))
            pick(1, lg, 1)
            nc.vector.tensor_tensor(hot_b[:], hot[:, 0], hot[:, 1], ALU.add).then_inc(hot_ready, 1)
            nc.vector.tensor_tensor(top[:, 3], top[:, 1], top[:, 0], ALU.subtract).then_inc(gap_ready, 1)
            dve.wait_ge(gap_exp, 1)
            order.then(nc.vector.tensor_scalar(top[:, 5], top[:, 4], 1.0, None, ALU.add))
            order.then(nc.vector.reciprocal(top[:, 6], top[:, 5]))
            order.then(nc.vector.tensor_scalar(top[:, 6], top[:, 6], gains[:, 1:2], None, ALU.mult))
            order.then(nc.vector.tensor_tensor(top[:, 7], top[:, 4], top[:, 6], ALU.mult))
            order.then(nc.vector.tensor_tensor(tmp[:], hot[:, 0], by_tile(top[:, 6]), ALU.mult))
            order.then(nc.vector.tensor_tensor(pos[:], hot[:, 1], by_tile(top[:, 7]), ALU.mult))
            dve.wait_ge(meta_set, 1)
            nc.vector.tensor_tensor(meta[:, :, 0:E], tmp[:], pos[:], ALU.add).then_inc(meta_set, 1)
            dve.wait_ge(ranks_done, 1)
            before = ps[:, 6, 0:TT * E].rearrange("p (t e) -> p t e", e=E)
            totals = ps[:, 6, TT * E:2 * TT * E].rearrange("p (t e) -> p t e", e=E)
            for e in range(E):
                last = nc.vector.tensor_tensor_scan(cum[:, :, e], ones_t[:], totals[:, :, e], 0.0, ALU.mult, ALU.add)
            order.then(last)
            order.then(nc.vector.tensor_tensor(pos[:], cum[:], totals, ALU.subtract))
            order.then(nc.vector.tensor_tensor(pos[:], pos[:], before, ALU.add))
            order.then(nc.vector.tensor_tensor(fill[:], cum[:, TT - 1, :].unsqueeze(2).broadcast_to([P, E, TT]),
                                               thresh[:].unsqueeze(1).broadcast_to([P, E, TT]), ALU.is_gt))
            order.then(nc.vector.tensor_reduce(per_e[:, 0], fill[:], AX.X, ALU.add))
            order.then(nc.vector.tensor_tensor_scan(per_e[:, 1], ones_t[:, 0:E], per_e[:, 0], 0.0, ALU.mult, ALU.add))
            order.then(nc.vector.tensor_tensor(per_e[:, 2], per_e[:, 1], per_e[:, 0], ALU.subtract))
            order.then(nc.vector.tensor_scalar(per_e[:, 3], per_e[:, 2], float(P), None, ALU.mult))
            order.then(nc.vector.tensor_tensor(pos[:], pos[:], by_expert(per_e[:, 3]), ALU.add))
            for k in range(TOP):
                order.then(nc.vector.tensor_tensor(tmp[:], pos[:], hot[:, k], ALU.mult))
                order.then(nc.vector.tensor_reduce(slot_f[:, k], tmp[:], AX.X, ALU.add))
            nc.vector.tensor_copy(slot_i[:], slot_f[:]).then_inc(routed, 1)
            order.then(nc.vector.tensor_tensor(past[:], count_f[:].unsqueeze(2).broadcast_to([P, NT, E]),
                                               per_e[:, 1].unsqueeze(1).broadcast_to([P, NT, E]), ALU.is_ge))
            order.then(nc.vector.tensor_reduce(tile_f[:], past[:], AX.X, ALU.add))
            order.then(nc.vector.tensor_scalar(tile_f[:], tile_f[:], float(E - 1), None, ALU.min))
            nc.vector.tensor_copy(tile_e[:], tile_f[:]).then_inc(routed, 1)

            def hid_product(n, p):
                dve.wait_ge(silu, n + 1)
                dve.wait_ge(up2, n + 1)
                wait_from(dve, hid_tr, n - 1)
                nc.vector.tensor_tensor(hid[:, p], act_g[:, p], ps[:, 2 + p], ALU.mult).then_inc(hid_ready, 1)

            def hid_low(n, p):
                dve.wait_ge(hid_hi, n + 1)
                nc.vector.tensor_tensor(hid_t[:, p, 1], ps[:, 4], hid_t[:, p, 0], ALU.subtract).then_inc(hid_lo, 1)

            def shared_y(n, p, half):
                dve.wait_ge(down_done, n + 1)
                wait_from(dve, y_out[p], 16 * half)
                nc.vector.scalar_tensor_tensor(y[:, p], ps[:, 5, 0:D], gains[:, 1:2],
                                               xs[:, at(n)].rearrange("p o d -> p (o d)"),
                                               ALU.mult, ALU.add).then_inc(y_ready, 1)

            def shared_step(n, p, half, with_piece=True):
                hid_product(n, p)
                if not isinstance(n, int) or n > 0:
                    shared_y(n - 1, 1 - p, half if p else half - 1)
                hid_low(n, p)
                if with_piece:
                    piece_low(n + 2, p)

            shared_step(0, 0, 0, False)
            shared_step(1, 1, 0)
            shared_step(2, 0, 1)
            looped(dve, 2, 3, PIECES - 2, shared_step)
            looped(dve, 2, PIECES - 2, TT - 1, lambda n, p, half: shared_step(n, p, half, False))
            shared_step(TT - 1, 1, (TT - 1) // 2, False)

            def expert_step(k, u, i):
                hid_product(TT + k, u % 2)
                if isinstance(k, int) and k == 0:
                    shared_y(TT - 1, 1, (TT - 1) // 2)
                hid_low(TT + k, u % 2)

            for k in range(4):
                expert_step(k, k, 0)
            looped(dve, 4, 4, NT - 3, expert_step)
            for k in range(NT - 3, NT):
                expert_step(k, k % 4, k // 4)

        @block.tensor
        def _(pe):
            pe.wait_ge(consts, 1)
            pe.wait_ge(gw_in, 32)
            for k in range(6):
                last = nc.tensor.transpose(ps[:, 5, 2 * NH * k:2 * NH * (k + 1)], gw_rows[:, P * k:P * (k + 1)],
                                           ident[0:2 * NH, 0:2 * NH])
            last.then_inc(gw_tr, 1)
            pe.wait_ge(gw_ready, 1)

            def gate_products(b, p):
                pe.wait_ge(lo_ready, 2 * b + 2)
                for t in range(TPB):
                    terms = [(w, l, c, g) for w in range(2) for c in range(C) for l, g in ((0, 0), (0, 1), (1, 0))]
                    for k, (w, l, c, g) in enumerate(terms):
                        last = nc.tensor.matmul(gates_ps[:, t, :, at(NH * b, NH)], split[:, p, w, l, c, P * t:P * (t + 1)],
                                                gw[:, w, g, c, :].rearrange("p (g h) -> p g h", g=2),
                                                start=k == 0, stop=k == len(terms) - 1)
                last.then_inc(gates_done, 1)

            def turn(b, u, i):
                p = u % 2
                wait_from(pe, lo_ready, 2 * b - 2)
                for done, src, bank in ((q_tr, qn[:, p], p), (k_tr, c_raw[:, u], 2 + p)):
                    if bank < 2:
                        pe.wait_ge(qn_ready, b + 1)
                    else:
                        pe.wait_ge(c_in[u], 16 * i + 16)
                    for t in range(TPB):
                        for c in range(C):
                            last = nc.tensor.transpose(ps[:, bank, S * c + P * t:S * c + P * (t + 1)],
                                                       src[:, t, P * c:P * (c + 1)], ident[:])
                    last.then_inc(done, 1)
                if not isinstance(b, int) or b > 0:
                    gate_products(b - 1, 1 - p)

            stepped(pe, 4, B, turn)
            gate_products(B - 1, (B - 1) % 2)

            pe.wait_ge(g_copied, 1)
            for g in range(2):
                for t in range(TPB):
                    last = nc.tensor.transpose(ps[:, 5, S * g + P * t:S * g + P * (t + 1)], g_tok[:, t, g, :], ident[:])
            last.then_inc(g_tr, 1)
            pe.wait_ge(en_ready, 1)
            for t in range(TPB):
                last = nc.tensor.transpose(ps[:, 6, P * t:P * (t + 1)], en_h[:, P * t:P * (t + 1)], ident[:])
            last.then_inc(en_tr, 1)
            pe.wait_ge(consts, 2)
            pe.wait_ge(v_ready, B)
            pe.wait_ge(lo_ready, 2 * B)
            pe.wait_ge(am_ready, 1)
            pe.wait_ge(en_tok, 1)

            def exponents(b, u, pair):
                n, q = NH // 2 * b + pair, pair % 2
                wait_from(pe, decay_ready, n - 1)
                for j in range(2):
                    h = 2 * pair + j
                    bank = ps[:, 2 * q + j]
                    nc.tensor.matmul(bank[:, 0:S], a_rows[:, u, h, 0:P], m_rows[:, u, h, :], start=True, stop=False,
                                     skip_group_check=True)
                    nc.tensor.matmul(bank[:, S:S + P], a_rows[:, u, h, P:S], m_rows[:, u, h, P:S], start=False,
                                     stop=False, skip_group_check=True)
                    for k in (0, 2):
                        last = nc.tensor.matmul(bank[:, P * k:P * (k + 1)], ident_b[:], causal[:], start=False,
                                                stop=True, skip_group_check=True)
                last.then_inc(arg_ready, 1)

            def scores(b, u, pair):
                n = NH // 2 * b + pair
                wait_from(pe, c_ready, n)
                for j in range(2):
                    h = 2 * pair + j
                    nc.tensor.matmul(ps[:, 4 + j, 0:S], ks[:, u, h, 0:P], qs[:, u, h, :], start=True, stop=True)
                    last = nc.tensor.matmul(ps[:, 4 + j, S:S + P], ks[:, u, h, P:S], qs[:, u, h, P:S], start=True, stop=True)
                last.then_inc(s_ready, 1)

            def heads(b, u, pair):
                n, q = NH // 2 * b + pair, pair % 2
                pe.wait_ge(c_ready, n + 1)
                if pair == 0:
                    wait_from(pe, h_read, b)
                for j in range(2):
                    h = 2 * pair + j
                    cols = slice((DH + 1) * h, (DH + 1) * (h + 1))
                    v0, v1 = (v_ext[:, at(TPB * b + t), h, :].rearrange("p o e -> p (o e)") for t in range(TPB))
                    nc.tensor.matmul(ps[:, 6, cols], cmat[:, q, j, 0:P], v0, start=True, stop=True)
                    nc.tensor.matmul(ps[:, 7, cols], cmat[:, q, j, P:S], v0, start=True, stop=False)
                    last = nc.tensor.matmul(ps[:, 7, cols], cmat[:, q, j, S:S + P], v1, start=False, stop=True)
                last.then_inc(h_ready, 1)

            def attend(b, u, i):
                pe.wait_ge(heads_in[u], 8 * 16 * (i + 1))
                exponents(b, u, 0)
                scores(b, u, 0)
                for pair in range(NH // 2):
                    if pair + 1 < NH // 2:
                        exponents(b, u, pair + 1)
                        scores(b, u, pair + 1)
                    heads(b, u, pair)

            stepped(pe, 2, B, attend)

            pe.wait_ge(rg_ready, 1)
            SPLIT = ((0, 0), (0, 1), (1, 0))

            def transpose_rows(bank, src):
                view = ps[:, bank, 0:D].bitcast(F16)
                for k in range(2 * C):
                    last = nc.tensor.transpose(view[:, P * k:P * (k + 1)], src[:, P * k:P * (k + 1)], ident_h[:])
                return last

            def logits(n, p):
                pe.wait_ge(row_copied, n + 1)
                terms = [(c, a, g) for c in range(C) for a, g in SPLIT]
                for k, (c, a, g) in enumerate(terms):
                    last = nc.tensor.matmul(ps[:, 6, at(E * n, E)], xt[:, p, D * a + P * c:D * a + P * (c + 1)],
                                            rg16[:, g, c, :], start=k == 0, stop=k == len(terms) - 1)
                last.then_inc(logits_done, 1)

            def row_turn(n, p, i):
                pe.wait_ge(xlo_ready, n + 1)
                wait_from(pe, row_copied, n - 1)
                transpose_rows(p, xr[:, at(n), 0:2 * D].rearrange("p o d -> p (o d)")).then_inc(row_tr, 1)
                if not isinstance(n, int) or n > 0:
                    logits(n - 1, 1 - p)

            stepped(pe, 2, TT, row_turn)
            logits(TT - 1, (TT - 1) % 2)
            pe.wait_ge(hot_ready, 1)
            pe.wait_ge(lg_read, 1)
            nc.tensor.matmul(ps[:, 6, 0:TT * E], earlier[:], hot_b[:].rearrange("p t e -> p (t e)"), start=True, stop=True)
            nc.tensor.matmul(ps[:, 6, TT * E:2 * TT * E], ones_b[:], hot_b[:].rearrange("p t e -> p (t e)"), start=True,
                             stop=True).then_inc(ranks_done, 1)

            def turn_x(n, src):
                wait_from(pe, xt_ready, n)
                transpose_rows(7, src).then_inc(x_tr, 1)

            def turn_own(n):
                turn_x(n, xr[:, at(n), 0:2 * D].rearrange("p o d -> p (o d)"))

            def turn_slots(k, u, i):
                pe.wait_ge(rows_in[u], 16 * i + 16)
                turn_x(TT + k, rows[:, u, 0:2 * D])

            def up(n, p, piece):
                pe.wait_ge(xt_ready, n + 1)
                wait_from(pe, hid_ready, n - 1)
                for m, done in ((0, up1), (1, up2)):
                    terms = [(c, a, g) for c in range(C) for a, g in SPLIT]
                    for k, (c, a, g) in enumerate(terms):
                        w = w16[:, at(piece + m), g, HID * c:HID * (c + 1)].rearrange("p o n -> p (o n)")
                        last = nc.tensor.matmul(ps[:, 2 * m + p], xt[:, p, D * a + P * c:D * a + P * (c + 1)], w,
                                                start=k == 0, stop=k == len(terms) - 1)
                    last.then_inc(done, 1)

            def down(n, p, piece):
                pe.wait_ge(hid_lo, n + 1)
                terms = [(c, a, g) for c in range(KH) for a, g in SPLIT]
                for k, (c, a, g) in enumerate(terms):
                    w = w16[:, at(piece + 2), g, D * c:D * (c + 1)].rearrange("p o n -> p (o n)")
                    last = nc.tensor.matmul(ps[:, 5, 0:D], hid_t[:, p, a, P * c:P * (c + 1)], w,
                                            start=k == 0, stop=k == len(terms) - 1)
                last.then_inc(down_done, 1)

            def turn_hid(n, p):
                pe.wait_ge(hid_ready, n + 1)
                wait_from(pe, hid_lo, n)
                for c in range(KH):
                    last = nc.tensor.transpose(ps[:, 4, P * c:P * (c + 1)], hid[:, p, P * c:P * (c + 1)], ident[:])
                last.then_inc(hid_tr, 1)

            def shared_step(n, p, half):
                up(n, p, 0)
                if not isinstance(n, int) or n < TT - 1:
                    turn_own(n + 1)
                else:
                    turn_slots(0, 0, 0)
                if not isinstance(n, int) or n > 0:
                    wait_from(pe, y_ready, n - 1)
                    down(n - 1, 1 - p, 0)
                turn_hid(n, p)

            pe.wait_ge(piece_lo, 3)
            pe.wait_ge(routed, 2)
            turn_own(0)
            for n in range(3):
                shared_step(n, n % 2, 0)
            looped(pe, 2, 3, TT - 1, shared_step)
            shared_step(TT - 1, 1, 0)

            def expert(k):
                return 3 + 3 * pe.value_load(tile_e[0:1, at(k)], min_val=0, max_val=E - 1)

            def expert_step(k, u, i):
                first, last = (isinstance(k, int) and k == n for n in (0, NT - 1))
                own, before = expert(k), None if first else expert(k - 1)
                up(TT + k, u % 2, own)
                if not last:
                    turn_slots(k + 1, (u + 1) % 4, i + (u + 1) // 4)
                if first:
                    pe.wait_ge(y_ready, TT - 1)
                    down(TT - 1, 1, 0)
                else:
                    if isinstance(k, int) and k == 1:
                        pe.wait_ge(y_ready, TT)
                    else:
                        pe.wait_ge(ye_ready, k - 1)
                    down(TT + k - 1, 1 - u % 2, before)
                turn_hid(TT + k, u % 2)

            pe.wait_ge(piece_lo, PIECES)
            for k in range(4):
                expert_step(k, k, 0)
            looped(pe, 4, 4, NT - 3, expert_step)
            for k in range(NT - 3, NT):
                expert_step(k, k % 4, k // 4)
            piece = expert(NT - 1)
            pe.wait_ge(ye_ready, NT - 1)
            down(TT + NT - 1, (NT - 1) % 2, piece)


_INS = ['x', 'ctx_1024', 'g_xattn', 'g_ffn', 'L0_xattn_igate_w', 'L0_xattn_igate_b', 'L0_xattn_fgate_w',
        'L0_xattn_fgate_b', 'L0_xattn_ln_scale', 'L0_ffn_gate_w', 'L0_ffn_ew1', 'L0_ffn_ew2', 'L0_ffn_ew3',
        'L0_ffn_sw1', 'L0_ffn_sw2', 'L0_ffn_sw3']


def kernel(**inputs):
    import numpy as _np
    import concourse.bacc as _bacc
    from concourse import mybir as _mybir
    from concourse.bass_utils import run_bass_kernel_spmd as _run

    nc = _bacc.Bacc("TRN2", target_bir_lowering=False, num_devices=1)
    arrays, args = {}, []
    for name in _INS:
        a = _np.ascontiguousarray(inputs[name])
        arrays[f"in_{name}_dram"] = a
        args.append(nc.dram_tensor(f"in_{name}_dram", a.shape, _mybir.dt.from_np(a.dtype), kind="ExternalInput").ap())
    b, s, d = inputs['x'].shape
    args.append(nc.dram_tensor("out_0_dram", (b * s + P, d), _mybir.dt.float32, kind="ExternalOutput").ap())
    flamingo_block(nc, *args)
    r = _run(nc, [arrays], core_ids=[0])
    return r.results[0]["out_0_dram"][:b * s].reshape(b, s, d)
```

```python
from contextlib import ExitStack

import concourse.bass as bass
from concourse import mybir

F32 = mybir.dt.float32
F16 = mybir.dt.float16
BF16 = mybir.dt.bfloat16
I32 = mybir.dt.int32
U32 = mybir.dt.uint32
ALU = mybir.AluOpType
ACT = mybir.ActivationFunctionType
AX = mybir.AxisListType

P = 128
LN_EPS = 1e-5
DEN_EPS = 1e-6
MASKED = -1e30


def at(n, count=1):
    return bass.ds(n, count)


def wait_from(eng, sem, value):
    if isinstance(value, int) and value <= 0:
        return
    eng.wait_ge(sem, value)


class Steps:

    def __init__(self, eng, sem, base=0):
        self.eng, self.sem, self.base, self.n = eng, sem, base, 0

    def then(self, instruction):
        instruction.then_inc(self.sem, 1)
        self.n += 1
        self.eng.wait_ge(self.sem, self.base + self.n)


def stepped(eng, unroll, total, step):
    for u in range(unroll):
        step(u, u, 0)
    with eng.Fori(1, total // unroll) as i:
        for u in range(unroll):
            step(unroll * i + u, u, i)


def looped(eng, unroll, first, end, step):
    with eng.Fori(0, (end - first) // unroll) as i:
        for u in range(unroll):
            step(unroll * i + (first + u), (first + u) % unroll, i + (first + u) // unroll)


def flamingo_block(nc, x, ctx_in, g_xattn, g_ffn, igate_w, igate_b, fgate_w, fgate_b, ln_scale,
                   gate_w, ew1, ew2, ew3, sw1, sw2, sw3, out):
    B, S, D = x.shape
    NH = igate_w.shape[0]
    DH = D // NH
    VW = DH + 2
    E = gate_w.shape[1]
    HID = ew1.shape[2]
    TPB = S // P
    TT = B * TPB
    C = D // P
    HPC = NH // C
    BH = B * NH
    assert BH == P and DH == 32 and HID == 4 * P and TPB == 2
    QK_SCALE = DH ** -0.5
    KH = HID // P
    PIECE = C * HID
    PIECES = 3 * (E + 1)
    TOP = 2
    NT = (TOP * TT * P + E * (P - 1)) // P
    ROW = 2 * D + 32

    es = ExitStack()
    with es:
        def sb(name, shape, dt, stack=es):
            return stack.enter_context(nc.sbuf_tensor(name, shape, dt))

        def sem(name):
            return es.enter_context(nc.semaphore(name))

        x_v = x.rearrange("b (t p) d -> p (b t) d", p=P)
        c_v = ctx_in.rearrange("b (t p) d -> p (b t) d", p=P)
        out_v = out[0:TT * P, :].rearrange("(t p) d -> p t d", p=P)
        qk = nc.dram_tensor("qk_split", [B, 2, 2, NH, DH, S], F16, kind="Internal").ap()
        slots = nc.dram_tensor("slots", [NT * P, ROW // 2], U32, kind="Internal").ap()
        am = nc.dram_tensor("gate_parts", [3, 2, BH, S], BF16, kind="Internal").ap()

        ident = sb("ident", [P, P], F32)
        ident_h = sb("ident_h", [P, P], F16)
        earlier = sb("earlier", [P, P], BF16)
        ones_b = sb("ones_b", [P, P], BF16)
        pad_row = sb("pad_row", [P, ROW // 2], U32)
        xs = sb("xs", [P, TT, D], F32)
        half = sb("half", [P, TT], F32)
        small = sb("small", [P, 8, TT], F32)
        mean = sb("mean", [P, TT], F32)
        rstd = sb("rstd", [P, TT], F32)
        stats = sb("stats", [P, TT, 6], F32)
        gains = sb("gains", [P, 2], F32)
        gains_in = sb("gains_in", [P, 2], F32)
        ps = es.enter_context(nc.psum_tensor("ps", [P, 8, 512], F32))

        early = ExitStack()
        with early:
            ln_gain = sb("ln_gain", [P, D], F32, early)
            ident_b = sb("ident_b", [P, P], BF16, early)
            causal = sb("causal", [P, P], BF16, early)
            v_ext = sb("v_ext", [P, 2, TT, NH, VW], F16, early)
            gw_rows = sb("gw_rows", [2 * NH, 3 * D], F32, early)
            gw_sum = sb("gw_sum", [P, 2, C, 2 * NH], F32, early)
            gw = sb("gw", [P, 2, 2, C, 2 * NH], F16, early)
            gw_tmp = sb("gw_tmp", [P, C, 2 * NH], F32, early)
            c_raw = sb("c_raw", [P, 4, TPB, D], F32, early)
            qn = sb("qn", [P, 2, TPB, D], F32, early)
            split = sb("split", [P, 2, 2, 2, C, S], F16, early)
            g_tok = sb("g_tok", [P, TPB, 2, BH], F32, early)
            bias = sb("bias", [P, 2], F32, early)
            ones = sb("ones", [P, S], F32, early)
            zf = sb("zf", [P, S], F32, early)
            zt = sb("zt", [P, S], F32, early)
            lf = sb("lf", [P, S], F32, early)
            cs = sb("cs", [P, S], F32, early)
            am32 = sb("am32", [P, 2, S], F32, early)
            am_r = sb("am_r", [P, 2, S], F32, early)
            am_p = sb("am_p", [P, 3, 2, S], BF16, early)
            nd = sb("nd", [P, S], F32, early)
            en_h = sb("en_h", [P, S], F32, early)
            en = sb("en", [P, TPB, BH], F32, early)
            ks = sb("ks", [3 * DH, 2, NH, S], F16, early)
            qs = sb("qs", [3 * DH, 2, NH, S], F16, early)
            a_rows = sb("a_rows", [6, 2, NH, S], BF16, early)
            m_rows = sb("m_rows", [6, 2, NH, S], BF16, early)
            decay = sb("decay", [P, 2, 2, 3 * P], F32, early)
            cmat = sb("cmat", [P, 2, 2, 3 * P], F32, early)
            c16 = sb("c16", [P, NH // 2, 2, 2, 3 * P], F16, early)
            den = sb("den", [P, 2, TPB, NH // 2], F32, early)
            offset = sb("offset", [P, TT], F32, early)
            hbuf = sb("hbuf", [P, TT, D], F32, early)

        w16 = sb("w16", [P, PIECES, 2, PIECE], F16)
        xr_w = sb("xr", [P, TT, ROW // 2], U32)
        xr = xr_w[:].bitcast(F16)
        stage = sb("stage", [P, 2, PIECE], F32)
        xt = sb("xt", [P, 2, 2 * D], F16)
        slot_i = sb("slot_i", [P, TOP, TT], U32)
        tile_e = sb("tile_e", [P, NT], I32)
        routing = ExitStack()
        with routing:
            xn = sb("xn", [P, 2, D], F32, routing)
            rg = sb("rg", [P, C, E], F32, routing)
            rg16 = sb("rg16", [P, 2, C, E], F16, routing)
            lg = sb("lg", [P, TT, E], F32, routing)
            hot = sb("hot", [P, TOP, TT, E], F32, routing)
            hot_b = sb("hot_b", [P, TT, E], BF16, routing)
            tmp = sb("tmp", [P, TT, E], F32, routing)
            pos = sb("pos", [P, TT, E], F32, routing)
            cum = sb("cum", [P, TT, E], F32, routing)
            top = sb("top", [P, 8, TT], F32, routing)
            slot_f = sb("slot_f", [P, TOP, TT], F32, routing)
            per_e = sb("per_e", [P, 4, E], F32, routing)
            fill = sb("fill", [P, E, TT], F32, routing)
            past = sb("past", [P, NT, E], F32, routing)
            tile_f = sb("tile_f", [P, NT], F32, routing)
            count_i = sb("count_i", [P, NT], I32, routing)
            count_f = sb("count_f", [P, NT], F32, routing)
            rev = sb("rev", [P, E], F32, routing)
            thresh = sb("thresh", [P, TT], F32, routing)
            ones_t = sb("ones_t", [P, TT], F32, routing)
        rows_w = sb("rows", [P, 4, ROW // 2], U32)
        rows = rows_w[:].bitcast(F16)
        act_g = sb("act_g", [P, 2, HID], F32)
        hid = sb("hid", [P, 2, HID], F32)
        hid_t = sb("hid_t", [P, 2, 2, HID], F16)
        y = sb("y", [P, 2, D], F32)
        meta = xr_w[:, :, D:ROW // 2].bitcast(F32)

        gates_ps = ps[:, 4, :].rearrange("p (t g n) -> p t g n", t=TPB, g=2)

        x_in = [sem(f"x_in{u}") for u in range(4)]
        c_in = [sem(f"c_in{u}") for u in range(4)]
        gw_in, vec_in = sem("gw_in"), sem("vec_in")
        consts, pool_step, half_set = sem("consts"), sem("pool_step"), sem("half_set")
        gw_tr, gw_ready = sem("gw_tr"), sem("gw_ready")
        var_ready, rstd_ready = sem("var_ready"), sem("rstd_ready")
        qn_ready, q_tr, k_tr, hi_ready, lo_ready = (sem(n) for n in ("qn_ready", "q_tr", "k_tr", "hi_ready", "lo_ready"))
        split_out = [sem(f"split_out{u}") for u in range(2)]
        gates_done, v_ready = sem("gates_done"), sem("v_ready")
        g_copied, g_tr, exp_ready, ln_ready, nabs_ready = (sem(n) for n in ("g_copied", "g_tr", "exp_ready", "ln_ready", "nabs_ready"))
        nd_ready, en_ready, en_tr, en_tok = (sem(n) for n in ("nd_ready", "en_ready", "en_tr", "en_tok"))
        am_ready, am_out = sem("am_ready"), sem("am_out")
        dve_a, dve_b, dve_c, dve_d = (sem(f"dve_{n}") for n in "abcd")
        heads_in = [sem(f"heads_in{u}") for u in range(2)]
        arg_ready, s_ready, decay_ready, c_ready, c_hi, c_lo, h_ready, h_read = (
            sem(n) for n in ("arg_ready", "s_ready", "decay_ready", "c_ready", "c_hi", "c_lo", "h_ready", "h_read"))
        gain_set = sem("gain_set")
        h_stats, v_hi, offset_ready, h_norm, h_gained = (
            sem(n) for n in ("h_stats", "v_hi", "offset_ready", "h_norm", "h_gained"))
        tanh_ready = sem("tanh_ready")
        pad_set, pad_out = sem("pad_set"), sem("pad_out")
        rg_in, rg_ready, numbers, floats = sem("rg_in"), sem("rg_ready"), sem("numbers"), sem("floats")
        xn_ready, xhi_ready, xlo_ready, row_tr, row_copied, logits_done = (
            sem(n) for n in ("xn_ready", "xhi_ready", "xlo_ready", "row_tr", "row_copied", "logits_done"))
        lg_read, gap_ready, gap_exp, hot_ready, ranks_done = (
            sem(n) for n in ("lg_read", "gap_ready", "gap_exp", "hot_ready", "ranks_done"))
        dve_e, routed, meta_set, scattered = sem("dve_e"), sem("routed"), sem("meta_set"), sem("scattered")
        stage_in = [sem(f"stage_in{u}") for u in range(2)]
        rows_in = [sem(f"rows_in{u}") for u in range(4)]
        piece_hi, piece_lo = sem("piece_hi"), sem("piece_lo")
        x_tr, xt_ready, up1, up2, silu, hid_ready, hid_tr, hid_hi, hid_lo, down_done = (
            sem(n) for n in ("x_tr", "xt_ready", "up1", "up2", "silu", "hid_ready", "hid_tr", "hid_hi", "hid_lo",
                             "down_done"))
        y_ready, y_out = sem("y_ready"), [sem(f"y_out{u}") for u in range(2)]
        ye_ready, add_turn, added = sem("ye_ready"), sem("add_turn"), sem("added")

        block = es.enter_context(nc.Block())

        @block.sync
        def _(sp):
            def load_x(b, u, i):
                wait_from(sp, x_in[u], 16 * i)
                sp.dma_start(xs[:, at(TPB * b, TPB)], x_v[:, at(TPB * b, TPB)]).then_inc(x_in[u], 16)

            def load_ctx(b, u, i):
                wait_from(sp, k_tr, b - 3)
                wait_from(sp, v_ready, b - 3)
                sp.dma_start(c_raw[:, u], c_v[:, at(TPB * b, TPB)]).then_inc(c_in[u], 16)

            stepped(sp, 4, B, load_x)
            stepped(sp, 4, B, load_ctx)

            sp.wait_ge(am_out, 16)
            sp.wait_ge(split_out[0], 16 * (B // 2))
            sp.wait_ge(split_out[1], 16 * (B // 2))

            def load_heads(b, u, i):
                wait_from(sp, s_ready, NH * (b - 1))
                for dst, which, parts in ((qs, 0, (0, 1, 0)), (ks, 1, (0, 0, 1))):
                    for r, part in enumerate(parts):
                        sp.dma_start(dst[DH * r:DH * (r + 1), u],
                                     qk[at(b), which, part].rearrange("o h d s -> d (o h) s")).then_inc(heads_in[u], 16)
                sp.dma_start(m_rows[0:3, u], am[:, 0, at(NH * b, NH), :]).then_inc(heads_in[u], 16)
                sp.dma_start(a_rows[3:6, u], am[:, 1, at(NH * b, NH), :]).then_inc(heads_in[u], 16)

            stepped(sp, 2, B, load_heads)

            def load_piece(src, slot):
                sp.dma_start(stage[:, slot], src).then_inc(stage_in[slot], 16)

            def expert_piece(e, m):
                w, chunks = ((ew1, C), (ew2, C), (ew3, KH))[m]
                return w[at(e)].rearrange("e (c p) n -> p (e c) n", c=chunks)

            sp.wait_ge(h_ready, NH // 2 * B)
            sp.wait_ge(dve_d, B)
            for k, w in enumerate((sw1, sw2, sw3)):
                wait_from(sp, piece_lo, k - 1)
                load_piece(w.rearrange("(c p) n -> p c n", p=P), k % 2)
            for k in (3, 4):
                sp.wait_ge(piece_lo, k - 1)
                load_piece(expert_piece(0, k - 3), k % 2)

            def store_shared(n, p):
                sp.wait_ge(y_ready, n + 1)
                sp.dma_start(out_v[:, at(n)], y[:, p:p + 1]).then_inc(y_out[p], 16)

            def shared_turn(n, u, e, m):
                store_shared(n - 1, (u - 1) % 2)
                sp.wait_ge(piece_lo, n + 3)
                load_piece(expert_piece(e, m), u % 2)

            with sp.Fori(0, 3) as i:
                for u in range(6):
                    shared_turn(6 * i + (u + 1), u + 1, 2 * i + (u + 2) // 3, (u + 2) % 3)
            for n in range(19, PIECES - 4):
                shared_turn(n, n, (n + 1) // 3, (n + 1) % 3)
            for n in range(PIECES - 4, TT - 1):
                store_shared(n - 1, (n - 1) % 2)

            sp.wait_ge(scattered, 16 * TOP * TT)

            def load_rows(k, u, i):
                wait_from(sp, added, 16 * (k - 3))
                sp.dma_start(rows_w[:, u], slots[at(P * k, P), :]).then_inc(rows_in[u], 16)

            for k in range(4):
                load_rows(k, k, 0)
            for n in (TT - 2, TT - 1):
                store_shared(n, n % 2)
            looped(sp, 4, 4, NT - 3, load_rows)
            for k in range(NT - 3, NT):
                load_rows(k, k % 4, k // 4)
            sp.wait_ge(added, 16 * NT)

        @block.gpsimd
        def _(pool):
            order = Steps(pool, pool_step)
            pool.dma_start(gw_rows[0:NH, :], igate_w).then_inc(gw_in, 16)
            pool.dma_start(gw_rows[NH:2 * NH, :], fgate_w).then_inc(gw_in, 16)
            pool.dma_start(gains_in[:, 0:1], g_xattn.unsqueeze(0).partition_broadcast(P)).then_inc(vec_in, 16)
            pool.dma_start(gains_in[:, 1:2], g_ffn.unsqueeze(0).partition_broadcast(P)).then_inc(vec_in, 16)
            pool.dma_start(ln_gain[:], ln_scale.unsqueeze(0).partition_broadcast(P)).then_inc(vec_in, 16)
            for b in range(B):
                pool.dma_start(bias[NH * b:NH * (b + 1), 0:1], igate_b.unsqueeze(1)).then_inc(vec_in, 16)
                pool.dma_start(bias[NH * b:NH * (b + 1), 1:2], fgate_b.unsqueeze(1)).then_inc(vec_in, 16)
            order.then(nc.gpsimd.memset(ident[:], 0.0))
            order.then(nc.gpsimd.affine_select(out=ident[:], in_=ident[:], compare_op=ALU.not_equal, fill=1.0,
                                               base=0, pattern=[[-1, P]], channel_multiplier=1))
            nc.gpsimd.tensor_copy(ident_h[:], ident[:])
            order.then(nc.gpsimd.memset(causal[:], 0.0))
            order.then(nc.gpsimd.affine_select(out=causal[:], in_=causal[:], compare_op=ALU.is_ge, fill=MASKED,
                                               base=0, pattern=[[1, P]], channel_multiplier=-1))
            nc.gpsimd.memset(ones[:], 1.0)
            nc.gpsimd.tensor_copy(ident_b[:], ident[:]).then_inc(consts, 1)
            order.then(nc.gpsimd.memset(earlier[:], 1.0))
            order.then(nc.gpsimd.affine_select(out=earlier[:], in_=earlier[:], compare_op=ALU.is_ge, fill=0.0,
                                               base=-1, pattern=[[1, P]], channel_multiplier=-1))
            nc.gpsimd.memset(ones_b[:], 1.0)
            order.then(nc.gpsimd.memset(pad_row[:], 0))
            nc.gpsimd.iota(pad_row[:, D + E:D + E + 1].bitcast(I32), pattern=[[0, 1]], base=TT * P,
                           channel_multiplier=1).then_inc(pad_set, 1)
            pool.wait_ge(pad_set, 1)
            pool.dma_start(slots.rearrange("(t p) r -> p t r", p=P),
                           pad_row[:].unsqueeze(1).broadcast_to([P, NT, ROW // 2])).then_inc(pad_out, 16)
            pool.dma_start(out[TT * P:TT * P + P, :], pad_row[:, 0:D].bitcast(F32)).then_inc(pad_out, 16)
            nc.gpsimd.memset(half[:], -0.5).then_inc(half_set, 1)
            pool.wait_ge(half_set, 1)
            nc.gpsimd.memset(a_rows[:], 1.0)
            nc.gpsimd.memset(m_rows[:], 1.0)
            nc.gpsimd.memset(v_ext[:, 0, :, :, DH:VW], 1.0)
            nc.gpsimd.memset(v_ext[:, 1, :, :, DH:VW], 0.0).then_inc(consts, 1)

            def reciprocal_root(n):
                pool.wait_ge(var_ready, n)
                nc.gpsimd.tensor_tensor(rstd[:], small[:, 6], half[:], ALU.pow).then_inc(rstd_ready, 1)

            reciprocal_root(1)

            def values(b, u, i):
                pool.wait_ge(c_in[u], 16 * i + 16)
                v = c_raw[:, u].rearrange("p t (h d) -> p t h d", h=NH)
                v_high, v_low = (v_ext[:, k, at(TPB * b, TPB), :, 0:DH] for k in range(2))
                nc.gpsimd.tensor_copy(v_high, v).then_inc(v_hi, 1)
                pool.wait_ge(v_hi, b + 1)
                nc.gpsimd.tensor_tensor(v_low, v, v_high, ALU.subtract).then_inc(v_ready, 1)

            stepped(pool, 4, B, values)
            pool.wait_ge(am_ready, 1)
            pool.dma_start(am.rearrange("a k n s -> n a k s"), am_p[:]).then_inc(am_out, 16)

            def mixed_low(b, u, i):
                for pair in range(NH // 2):
                    pool.wait_ge(c_hi, NH // 2 * b + pair + 1)
                    nc.gpsimd.tensor_tensor(c16[:, pair, 1], cmat[:, pair % 2], c16[:, pair, 0],
                                            ALU.subtract).then_inc(c_lo, 1)

            stepped(pool, 2, B, mixed_low)
            reciprocal_root(2)

            def gain(b, u, i):
                h_b = hbuf[:, at(TPB * b, TPB)]
                pool.wait_ge(h_norm, b + 1)
                nc.gpsimd.tensor_tensor(h_b, h_b, ln_gain[:].unsqueeze(1).broadcast_to([P, TPB, D]),
                                        ALU.mult).then_inc(h_gained, 1)

            pool.wait_ge(gain_set, 1)
            stepped(pool, 2, B, gain)
            pool.wait_ge(h_ready, NH // 2 * B)
            pool.wait_ge(dve_d, B)
            for c in range(C):
                pool.dma_start(rg[:, c], gate_w[P * c:P * (c + 1), :]).then_inc(rg_in, 16)

            def number(dst, columns, pattern, base):
                order.then(nc.gpsimd.iota(count_i[:, 0:columns], pattern=pattern, base=base, channel_multiplier=0))
                order.then(nc.gpsimd.tensor_copy(dst, count_i[:, 0:columns]))

            number(rev[:], E, [[-1, E]], E)
            number(thresh[:], TT, [[P, TT]], 0)
            number(count_f[:], NT, [[1, NT]], 0)
            nc.gpsimd.memset(ones_t[:], 1.0).then_inc(numbers, 1)
            reciprocal_root(3)
            order.then(nc.gpsimd.memset(meta, 0.0))
            nc.gpsimd.iota(xr_w[:, :, D + E:D + E + 1].bitcast(I32), pattern=[[P, TT], [0, 1]], base=0,
                           channel_multiplier=1).then_inc(meta_set, 1)

            pool.wait_ge(routed, 1)
            pool.wait_ge(meta_set, 2)
            pool.wait_ge(pad_out, 32)
            for k in range(TOP):
                for t in range(TT):
                    nc.gpsimd.indirect_dma_start(
                        out=slots, out_offset=bass.IndirectOffsetOnAxis(ap=slot_i[:, k, t:t + 1], axis=0),
                        in_=xr_w[:, t, :], in_offset=None).then_inc(scattered, 16)

            for p in range(2):
                pool.wait_ge(y_out[p], 16 * TT // 2)

            def add_rows(k, u, i):
                pool.wait_ge(ye_ready, k + 1)
                wait_from(pool, added, 16 * k)
                pool.sem_inc(add_turn, 1)
                nc.gpsimd.indirect_dma_start(
                    out=out, out_offset=bass.IndirectOffsetOnAxis(
                        ap=rows_w[:, u, D + E:D + E + 1], axis=0),
                    in_=y[:, u % 2], in_offset=None, compute_op=ALU.add).then_inc(added, 16)

            for k in range(4):
                add_rows(k, k, 0)
            looped(pool, 4, 4, NT - 3, add_rows)
            for k in range(NT - 3, NT):
                add_rows(k, k % 4, k // 4)

        @block.scalar
        def _(act):
            act.wait_ge(vec_in, 16 * (3 + 2 * B))
            nc.scalar.activation(gains[:], gains_in[:], ACT.Tanh).then_inc(tanh_ready, 1)

            def store_split(b, p):
                act.wait_ge(lo_ready, 2 * b + 2)
                act.dma_start(qk[at(b)].rearrange("o w l (c g) d s -> (g d) (o w l) c s", c=C),
                              split[:, p].rearrange("p w l c s -> p (w l) c s")).then_inc(split_out[p], 16)

            def high(b, u, i):
                p = u % 2
                wait_from(act, split_out[p], 32 * i + 16 * (u // 2))
                wait_from(act, gates_done, b - 1)
                act.wait_ge(q_tr, b + 1)
                nc.scalar.activation(split[:, p, 0, 0], ps[:, p], ACT.Copy).then_inc(hi_ready, 1)
                act.wait_ge(k_tr, b + 1)
                nc.scalar.activation(split[:, p, 1, 0], ps[:, 2 + p], ACT.Copy).then_inc(hi_ready, 1)
                if not isinstance(b, int) or b > 0:
                    store_split(b - 1, 1 - p)

            stepped(act, 4, B, high)
            store_split(B - 1, (B - 1) % 2)

            act.wait_ge(nabs_ready, 1)
            nc.scalar.activation(zt[:], zt[:], ACT.Exp).then_inc(exp_ready, 1)
            act.wait_ge(exp_ready, 1)
            nc.scalar.activation(zt[:], zt[:], ACT.Ln, bias=1.0).then_inc(ln_ready, 1)
            act.wait_ge(nd_ready, 1)
            nc.scalar.activation(en_h[:], nd[:], ACT.Exp, scale=-1.0).then_inc(en_ready, 1)

            def decays(n, q):
                act.wait_ge(arg_ready, n + 1)
                wait_from(act, c_ready, 2 * (n - 1))
                nc.scalar.activation(decay[:, q], ps[:, 2 * q:2 * q + 2, 0:3 * P], ACT.Exp).then_inc(decay_ready, 1)

            def mixed_high(n, pair):
                act.wait_ge(c_ready, 2 * n + 2)
                wait_from(act, h_ready, n - 3)
                nc.scalar.activation(c16[:, pair, 0], cmat[:, pair % 2], ACT.Copy).then_inc(c_hi, 1)

            def decays_and_high(b, u, i):
                for pair in range(NH // 2):
                    n = NH // 2 * b + pair
                    decays(n, pair % 2)
                    if pair or not isinstance(b, int) or b > 0:
                        mixed_high(n - 1, (pair - 1) % (NH // 2))

            stepped(act, 2, B, decays_and_high)
            mixed_high(NH // 2 * B - 1, NH // 2 - 1)

            act.wait_ge(offset_ready, 1)

            def normal(b, u, i):
                for t in range(TPB):
                    h_n = hbuf[:, at(TPB * b + t)].rearrange("p o d -> p (o d)")
                    last = nc.scalar.activation(h_n, h_n, ACT.Identity, bias=offset[:, at(TPB * b + t)],
                                                scale=rstd[:, at(TPB * b + t)])
                last.then_inc(h_norm, 1)

            stepped(act, 2, B, normal)

            def piece_high(k, slot, turn):
                act.wait_ge(stage_in[slot], 16 * turn + 16)
                nc.scalar.activation(w16[:, at(k), 0].rearrange("p o n -> p (o n)"), stage[:, slot],
                                     ACT.Copy).then_inc(piece_hi, 1)

            for k in range(3):
                piece_high(k, k % 2, k // 2)

            def copy_rows(n, p):
                act.wait_ge(row_tr, n + 1)
                wait_from(act, logits_done, n - 1)
                nc.scalar.activation(xt[:, p], ps[:, p, 0:D].bitcast(F16), ACT.Copy).then_inc(row_copied, 1)

            def row_high(n, p, i):
                act.wait_ge(xn_ready, n + 1)
                nc.scalar.activation(xr[:, at(n), 0:D].rearrange("p o d -> p (o d)"), xn[:, p], ACT.Copy).then_inc(xhi_ready, 1)
                if not isinstance(n, int) or n > 0:
                    copy_rows(n - 1, 1 - p)

            stepped(act, 2, TT, row_high)
            copy_rows(TT - 1, (TT - 1) % 2)
            act.wait_ge(gap_ready, 1)
            nc.scalar.activation(top[:, 4], top[:, 3], ACT.Exp).then_inc(gap_exp, 1)

            def copy_x(n, p):
                act.wait_ge(x_tr, n + 1)
                wait_from(act, up2, n - 1)
                nc.scalar.activation(xt[:, p], ps[:, 7, 0:D].bitcast(F16), ACT.Copy).then_inc(xt_ready, 1)

            def gate_silu(n, p):
                act.wait_ge(up1, n + 1)
                wait_from(act, hid_ready, n - 1)
                nc.scalar.activation(act_g[:, p], ps[:, p], ACT.Silu).then_inc(silu, 1)

            def hid_high(n, p):
                act.wait_ge(hid_tr, n + 1)
                wait_from(act, down_done, n - 1)
                nc.scalar.activation(hid_t[:, p, 0], ps[:, 4], ACT.Copy).then_inc(hid_hi, 1)

            def expert_y(k, u, i):
                e = act.value_load(tile_e[0:1, at(k)], min_val=0, max_val=E - 1)
                act.wait_ge(down_done, TT + k + 1)
                act.wait_ge(rows_in[u], 16 * i + 16)
                if isinstance(k, int) and k < 2:
                    act.wait_ge(y_out[k], 16 * (TT // 2))
                wait_from(act, added, 16 * (k - 1))
                nc.scalar.activation(y[:, u % 2], ps[:, 5, 0:D], ACT.Copy,
                                     scale=rows_w[:, u, D:D + E].bitcast(F32)[:, at(e)]).then_inc(ye_ready, 1)

            def shared_step(n, p, half, with_piece=True):
                gate_silu(n, p)
                copy_x(n + 1, 1 - p)
                hid_high(n, p)
                if with_piece:
                    piece_high(n + 2, p, half + 1)

            copy_x(0, 0)
            shared_step(0, 0, 0, False)
            shared_step(1, 1, 0)
            shared_step(2, 0, 1)
            looped(act, 2, 3, PIECES - 2, shared_step)
            looped(act, 2, PIECES - 2, TT - 1, lambda n, p, half: shared_step(n, p, half, False))
            shared_step(TT - 1, 1, 0, False)

            def expert_step(k, u, i, last=False):
                gate_silu(TT + k, u % 2)
                if not last:
                    copy_x(TT + k + 1, 1 - u % 2)
                if not isinstance(k, int) or k > 0:
                    expert_y(k - 1, (u - 1) % 4, i if u else i - 1)
                hid_high(TT + k, u % 2)

            for k in range(4):
                expert_step(k, k, 0)
            looped(act, 4, 4, NT - 3, expert_step)
            for k in range(NT - 3, NT):
                expert_step(k, k % 4, k // 4, k == NT - 1)
            expert_y(NT - 1, (NT - 1) % 4, (NT - 1) // 4)

        @block.vector
        def _(dve):
            order = Steps(dve, dve_a)
            dve.wait_ge(gw_tr, 1)
            wt = ps[:, 5, 0:6 * 2 * NH].rearrange("p (k n) -> p k n", k=6)
            nc.vector.tensor_copy(gw_sum[:, 0], wt[:, 0:2])
            order.then(nc.vector.tensor_copy(gw_tmp[:], wt[:, 2:4]))
            order.then(nc.vector.tensor_tensor(gw_sum[:, 1], gw_tmp[:], wt[:, 4:6], ALU.add))
            order.then(nc.vector.tensor_copy(gw[:, :, 0], gw_sum[:]))
            nc.vector.tensor_tensor(gw[:, :, 1], gw_sum[:], gw[:, :, 0], ALU.subtract).then_inc(gw_ready, 1)

            def layer_stats(n):
                me, mo, ve, vo = (stats[:, :, k] for k in (1, 4, 2, 5))
                nc.vector.tensor_tensor(small[:, 0], me, mo, ALU.add)
                nc.vector.tensor_tensor(small[:, 1], me, mo, ALU.subtract)
                order.then(nc.vector.tensor_tensor(small[:, 2], ve, vo, ALU.add))
                nc.vector.tensor_scalar(mean[:], small[:, 0], 0.5, None, ALU.mult)
                order.then(nc.vector.scalar_tensor_tensor(small[:, 3], small[:, 1], 0.25, small[:, 1], ALU.mult, ALU.mult))
                order.then(nc.vector.scalar_tensor_tensor(small[:, 4], small[:, 2], 1.0 / D, small[:, 3], ALU.mult, ALU.add))
                nc.vector.tensor_scalar(small[:, 6], small[:, 4], LN_EPS, None, ALU.add).then_inc(var_ready, 1)
                dve.wait_ge(rstd_ready, n)

            def x_stats(b, u, i):
                dve.wait_ge(x_in[u], 16 * i + 16)
                for t in range(TPB):
                    nc.vector.bn_stats(stats[:, at(TPB * b + t)], xs[:, at(TPB * b + t)])

            stepped(dve, 4, B, x_stats)
            order.then(nc.vector.memset(small[:, 7], 0.0))
            layer_stats(1)

            def queries(b, u, i):
                p = u % 2
                wait_from(dve, q_tr, b - 1)
                for t in range(TPB):
                    n = TPB * b + t
                    last = nc.vector.tensor_scalar(qn[:, p, t], xs[:, at(n)].rearrange("p o d -> p (o d)"),
                                                   mean[:, at(n)], rstd[:, at(n)], ALU.subtract, ALU.mult)
                last.then_inc(qn_ready, 1)

            def low(b, u, i):
                p = u % 2
                for w in range(2):
                    dve.wait_ge(hi_ready, 2 * b + w + 1)
                    nc.vector.tensor_tensor(split[:, p, w, 1].rearrange("p c s -> p (c s)"), ps[:, 2 * w + p],
                                            split[:, p, w, 0].rearrange("p c s -> p (c s)"),
                                            ALU.subtract).then_inc(lo_ready, 1)

            def queries_and_low(b, u, i):
                queries(b, u, i)
                low(b, u, i)

            stepped(dve, 4, B, queries_and_low)

            dve.wait_ge(gates_done, B)
            nc.vector.tensor_copy(g_tok[:].rearrange("p t g n -> p (t g n)"), ps[:, 4]).then_inc(g_copied, 1)
            dve.wait_ge(g_tr, 1)
            dve.wait_ge(vec_in, 16 * (3 + 2 * B))
            ig, fg = ps[:, 5, 0:S], ps[:, 5, S:2 * S]
            order.then(nc.vector.tensor_scalar(zf[:], fg, bias[:, 1:2], None, ALU.add))
            order.then(nc.vector.scalar_tensor_tensor(zt[:], zf[:], -1.0, zf[:], ALU.mult, ALU.min))
            nc.vector.tensor_scalar(zf[:], zf[:], 0.0, None, ALU.min).then_inc(nabs_ready, 1)
            dve.wait_ge(ln_ready, 1)
            order.then(nc.vector.tensor_tensor(lf[:], zf[:], zt[:], ALU.subtract))
            order.then(nc.vector.tensor_tensor_scan(cs[:], ones[:], lf[:], 0.0, ALU.mult, ALU.add))
            order.then(nc.vector.scalar_tensor_tensor(am32[:, 1], ig, bias[:, 0:1], cs[:], ALU.add, ALU.subtract))
            order.then(nc.vector.tensor_tensor_scan(lf[:], am32[:, 1], am32[:, 1], -3e38, ALU.max, ALU.max))
            nc.vector.tensor_tensor(nd[:], cs[:], lf[:], ALU.add).then_inc(nd_ready, 1)
            order.then(nc.vector.tensor_scalar(am32[:, 0], lf[:], -1.0, None, ALU.mult))
            order.then(nc.vector.tensor_copy(am_p[:, 0], am32[:]))
            order.then(nc.vector.tensor_tensor(am_r[:], am32[:], am_p[:, 0], ALU.subtract))
            order.then(nc.vector.tensor_copy(am_p[:, 1], am_r[:]))
            order.then(nc.vector.tensor_tensor(am32[:], am_r[:], am_p[:, 1], ALU.subtract))
            nc.vector.tensor_copy(am_p[:, 2], am32[:]).then_inc(am_ready, 1)
            dve.wait_ge(en_tr, 1)
            nc.vector.tensor_scalar(en[:].rearrange("p t n -> p (t n)"), ps[:, 6, 0:S], DEN_EPS, None,
                                    ALU.add).then_inc(en_tok, 1)
            dve.wait_ge(en_tok, 1)

            def mix(n, q):
                dve.wait_ge(decay_ready, n + 1)
                wait_from(dve, c_lo, n - 1)
                for j in range(2):
                    dve.wait_ge(s_ready, 2 * n + j + 1)
                    nc.vector.scalar_tensor_tensor(cmat[:, q, j], ps[:, 4 + j, 0:3 * P], QK_SCALE, decay[:, q, j],
                                                   ALU.mult, ALU.mult).then_inc(c_ready, 1)

            def divide(b, side):
                m = 2 * b + side
                chain = Steps(dve, dve_c, 4 * m)
                dve.wait_ge(h_ready, 2 * (m + 1))
                h_ps = ps[:, 6 + side, 0:TPB * (NH // 2) * (DH + 1)].rearrange("p (t h e) -> p t h e", t=TPB, h=NH // 2)
                h_sb = hbuf[:, at(TPB * b, TPB)].rearrange("p t (h d) -> p t h d", h=NH)
                heads = slice(NH // 2 * side, NH // 2 * (side + 1))
                chain.then(nc.vector.tensor_copy(den[:, 0], h_ps[:, :, :, DH]))
                chain.then(nc.vector.scalar_tensor_tensor(den[:, 1], den[:, 0], -1.0, den[:, 0], ALU.mult, ALU.max))
                chain.then(nc.vector.scalar_tensor_tensor(
                    den[:, 0], den[:, 1], DEN_EPS, en[:, :, at(NH * b + NH // 2 * side, NH // 2)], ALU.add, ALU.max))
                chain.then(nc.vector.reciprocal(den[:, 1], den[:, 0]))
                nc.vector.tensor_tensor(h_sb[:, :, heads], h_ps[:, :, :, 0:DH],
                                        den[:, 1].unsqueeze(3).broadcast_to([P, TPB, NH // 2, DH]),
                                        ALU.mult).then_inc(h_read, 1)

            def head_stats(b):
                dve.wait_ge(h_read, 2 * b + 2)
                for t in range(TPB):
                    last = nc.vector.bn_stats(stats[:, at(TPB * b + t)], hbuf[:, at(TPB * b + t)])
                last.then_inc(h_stats, 1)

            def mix_and_divide(b, u, i):
                later = not isinstance(b, int) or b > 0
                for pair in range(NH // 2):
                    mix(NH // 2 * b + pair, pair % 2)
                    if later and pair % 2 == 0:
                        divide(b - 1, pair // 2)
                    if later and pair == NH // 2 - 1:
                        head_stats(b - 1)

            stepped(dve, 2, B, mix_and_divide)
            for side in range(2):
                divide(B - 1, side)
            head_stats(B - 1)

            dve.wait_ge(h_stats, B)
            dve.wait_ge(tanh_ready, 1)
            nc.vector.tensor_scalar(ln_gain[:], ln_gain[:], gains[:, 0:1], None, ALU.mult).then_inc(gain_set, 1)
            layer_stats(2)
            nc.vector.scalar_tensor_tensor(offset[:], mean[:], -1.0, rstd[:], ALU.mult, ALU.mult).then_inc(offset_ready, 1)

            def residual(b):
                x_b = xs[:, at(TPB * b, TPB)]
                dve.wait_ge(h_gained, b + 1)
                nc.vector.tensor_tensor(x_b, x_b, hbuf[:, at(TPB * b, TPB)], ALU.add).then_inc(dve_d, 1)

            def x1_stats(b):
                dve.wait_ge(dve_d, b + 1)
                for t in range(TPB):
                    last = nc.vector.bn_stats(stats[:, at(TPB * b + t)], xs[:, at(TPB * b + t)])
                last.then_inc(h_stats, 1)

            def residual_and_stats(b, u, i):
                residual(b)
                if not isinstance(b, int) or b > 0:
                    x1_stats(b - 1)

            stepped(dve, 2, B, residual_and_stats)
            x1_stats(B - 1)
            dve.wait_ge(h_stats, 2 * B)
            layer_stats(3)
            dve.wait_ge(rg_in, 16 * C)
            order.then(nc.vector.tensor_copy(rg16[:, 0], rg[:]))
            nc.vector.tensor_tensor(rg16[:, 1], rg[:], rg16[:, 0], ALU.subtract).then_inc(rg_ready, 1)

            def piece_low(k, slot):
                dve.wait_ge(piece_hi, k + 1)
                nc.vector.tensor_tensor(w16[:, at(k), 1].rearrange("p o n -> p (o n)"), stage[:, slot],
                                        w16[:, at(k), 0].rearrange("p o n -> p (o n)"), ALU.subtract).then_inc(piece_lo, 1)

            for k in range(3):
                piece_low(k, k % 2)

            def row_low(n, p):
                dve.wait_ge(xhi_ready, n + 1)
                nc.vector.tensor_tensor(xr[:, at(n), D:2 * D].rearrange("p o d -> p (o d)"), xn[:, p],
                                        xr[:, at(n), 0:D].rearrange("p o d -> p (o d)"), ALU.subtract).then_inc(xlo_ready, 1)

            def normalise(n, p, i):
                wait_from(dve, xlo_ready, n - 1)
                nc.vector.tensor_scalar(xn[:, p], xs[:, at(n)].rearrange("p o d -> p (o d)"), mean[:, at(n)],
                                        rstd[:, at(n)], ALU.subtract, ALU.mult).then_inc(xn_ready, 1)
                if not isinstance(n, int) or n > 0:
                    row_low(n - 1, 1 - p)

            stepped(dve, 2, TT, normalise)
            row_low(TT - 1, (TT - 1) % 2)

            dve.wait_ge(numbers, 1)
            dve.wait_ge(logits_done, TT)
            by_tile = lambda a: a.unsqueeze(2).broadcast_to([P, TT, E])
            by_expert = lambda a: a.unsqueeze(1).broadcast_to([P, TT, E])
            nc.vector.tensor_copy(lg[:].rearrange("p t e -> p (t e)"), ps[:, 6, 0:TT * E]).then_inc(lg_read, 1)
            dve.wait_ge(lg_read, 1)

            def pick(k, values, best):
                order.then(nc.vector.tensor_reduce(top[:, best], values[:], AX.X, ALU.max))
                order.then(nc.vector.tensor_tensor(tmp[:], values[:], by_tile(top[:, best]), ALU.is_equal))
                order.then(nc.vector.tensor_tensor(tmp[:], tmp[:], by_expert(rev[:]), ALU.mult))
                order.then(nc.vector.tensor_reduce(top[:, 2], tmp[:], AX.X, ALU.max))
                order.then(nc.vector.tensor_tensor(hot[:, k], tmp[:], by_tile(top[:, 2]), ALU.is_equal))

            pick(0, lg, 0)
            order.then(nc.vector.scalar_tensor_tensor(lg[:], hot[:, 0], -3e38, lg[:], ALU.mult, ALU.add))
            pick(1, lg, 1)
            nc.vector.tensor_tensor(hot_b[:], hot[:, 0], hot[:, 1], ALU.add).then_inc(hot_ready, 1)
            nc.vector.tensor_tensor(top[:, 3], top[:, 1], top[:, 0], ALU.subtract).then_inc(gap_ready, 1)
            dve.wait_ge(gap_exp, 1)
            order.then(nc.vector.tensor_scalar(top[:, 5], top[:, 4], 1.0, None, ALU.add))
            order.then(nc.vector.reciprocal(top[:, 6], top[:, 5]))
            order.then(nc.vector.tensor_scalar(top[:, 6], top[:, 6], gains[:, 1:2], None, ALU.mult))
            order.then(nc.vector.tensor_tensor(top[:, 7], top[:, 4], top[:, 6], ALU.mult))
            order.then(nc.vector.tensor_tensor(tmp[:], hot[:, 0], by_tile(top[:, 6]), ALU.mult))
            order.then(nc.vector.tensor_tensor(pos[:], hot[:, 1], by_tile(top[:, 7]), ALU.mult))
            dve.wait_ge(meta_set, 1)
            nc.vector.tensor_tensor(meta[:, :, 0:E], tmp[:], pos[:], ALU.add).then_inc(meta_set, 1)
            dve.wait_ge(ranks_done, 1)
            before = ps[:, 6, 0:TT * E].rearrange("p (t e) -> p t e", e=E)
            totals = ps[:, 6, TT * E:2 * TT * E].rearrange("p (t e) -> p t e", e=E)
            for e in range(E):
                last = nc.vector.tensor_tensor_scan(cum[:, :, e], ones_t[:], totals[:, :, e], 0.0, ALU.mult, ALU.add)
            order.then(last)
            order.then(nc.vector.tensor_tensor(pos[:], cum[:], totals, ALU.subtract))
            order.then(nc.vector.tensor_tensor(pos[:], pos[:], before, ALU.add))
            order.then(nc.vector.tensor_tensor(fill[:], cum[:, TT - 1, :].unsqueeze(2).broadcast_to([P, E, TT]),
                                               thresh[:].unsqueeze(1).broadcast_to([P, E, TT]), ALU.is_gt))
            order.then(nc.vector.tensor_reduce(per_e[:, 0], fill[:], AX.X, ALU.add))
            order.then(nc.vector.tensor_tensor_scan(per_e[:, 1], ones_t[:, 0:E], per_e[:, 0], 0.0, ALU.mult, ALU.add))
            order.then(nc.vector.tensor_tensor(per_e[:, 2], per_e[:, 1], per_e[:, 0], ALU.subtract))
            order.then(nc.vector.tensor_scalar(per_e[:, 3], per_e[:, 2], float(P), None, ALU.mult))
            order.then(nc.vector.tensor_tensor(pos[:], pos[:], by_expert(per_e[:, 3]), ALU.add))
            for k in range(TOP):
                order.then(nc.vector.tensor_tensor(tmp[:], pos[:], hot[:, k], ALU.mult))
                order.then(nc.vector.tensor_reduce(slot_f[:, k], tmp[:], AX.X, ALU.add))
            nc.vector.tensor_copy(slot_i[:], slot_f[:]).then_inc(routed, 1)
            order.then(nc.vector.tensor_tensor(past[:], count_f[:].unsqueeze(2).broadcast_to([P, NT, E]),
                                               per_e[:, 1].unsqueeze(1).broadcast_to([P, NT, E]), ALU.is_ge))
            order.then(nc.vector.tensor_reduce(tile_f[:], past[:], AX.X, ALU.add))
            order.then(nc.vector.tensor_scalar(tile_f[:], tile_f[:], float(E - 1), None, ALU.min))
            nc.vector.tensor_copy(tile_e[:], tile_f[:]).then_inc(routed, 1)

            def hid_product(n, p):
                dve.wait_ge(silu, n + 1)
                dve.wait_ge(up2, n + 1)
                wait_from(dve, hid_tr, n - 1)
                nc.vector.tensor_tensor(hid[:, p], act_g[:, p], ps[:, 2 + p], ALU.mult).then_inc(hid_ready, 1)

            def hid_low(n, p):
                dve.wait_ge(hid_hi, n + 1)
                nc.vector.tensor_tensor(hid_t[:, p, 1], ps[:, 4], hid_t[:, p, 0], ALU.subtract).then_inc(hid_lo, 1)

            def shared_y(n, p, half):
                dve.wait_ge(down_done, n + 1)
                wait_from(dve, y_out[p], 16 * half)
                nc.vector.scalar_tensor_tensor(y[:, p], ps[:, 5, 0:D], gains[:, 1:2],
                                               xs[:, at(n)].rearrange("p o d -> p (o d)"),
                                               ALU.mult, ALU.add).then_inc(y_ready, 1)

            def shared_step(n, p, half, with_piece=True):
                hid_product(n, p)
                if not isinstance(n, int) or n > 0:
                    shared_y(n - 1, 1 - p, half if p else half - 1)
                hid_low(n, p)
                if with_piece:
                    piece_low(n + 2, p)

            shared_step(0, 0, 0, False)
            shared_step(1, 1, 0)
            shared_step(2, 0, 1)
            looped(dve, 2, 3, PIECES - 2, shared_step)
            looped(dve, 2, PIECES - 2, TT - 1, lambda n, p, half: shared_step(n, p, half, False))
            shared_step(TT - 1, 1, (TT - 1) // 2, False)

            def expert_step(k, u, i):
                hid_product(TT + k, u % 2)
                if isinstance(k, int) and k == 0:
                    shared_y(TT - 1, 1, (TT - 1) // 2)
                hid_low(TT + k, u % 2)

            for k in range(4):
                expert_step(k, k, 0)
            looped(dve, 4, 4, NT - 3, expert_step)
            for k in range(NT - 3, NT):
                expert_step(k, k % 4, k // 4)

        @block.tensor
        def _(pe):
            pe.wait_ge(consts, 1)
            pe.wait_ge(gw_in, 32)
            for k in range(6):
                last = nc.tensor.transpose(ps[:, 5, 2 * NH * k:2 * NH * (k + 1)], gw_rows[:, P * k:P * (k + 1)],
                                           ident[0:2 * NH, 0:2 * NH])
            last.then_inc(gw_tr, 1)
            pe.wait_ge(gw_ready, 1)

            def gate_products(b, p):
                pe.wait_ge(lo_ready, 2 * b + 2)
                for t in range(TPB):
                    terms = [(w, l, c, g) for w in range(2) for c in range(C) for l, g in ((0, 0), (0, 1), (1, 0))]
                    for k, (w, l, c, g) in enumerate(terms):
                        last = nc.tensor.matmul(gates_ps[:, t, :, at(NH * b, NH)], split[:, p, w, l, c, P * t:P * (t + 1)],
                                                gw[:, w, g, c, :].rearrange("p (g h) -> p g h", g=2),
                                                start=k == 0, stop=k == len(terms) - 1)
                last.then_inc(gates_done, 1)

            def turn(b, u, i):
                p = u % 2
                wait_from(pe, lo_ready, 2 * b - 2)
                for done, src, bank in ((q_tr, qn[:, p], p), (k_tr, c_raw[:, u], 2 + p)):
                    if bank < 2:
                        pe.wait_ge(qn_ready, b + 1)
                    else:
                        pe.wait_ge(c_in[u], 16 * i + 16)
                    for t in range(TPB):
                        for c in range(C):
                            last = nc.tensor.transpose(ps[:, bank, S * c + P * t:S * c + P * (t + 1)],
                                                       src[:, t, P * c:P * (c + 1)], ident[:])
                    last.then_inc(done, 1)
                if not isinstance(b, int) or b > 0:
                    gate_products(b - 1, 1 - p)

            stepped(pe, 4, B, turn)
            gate_products(B - 1, (B - 1) % 2)

            pe.wait_ge(g_copied, 1)
            for g in range(2):
                for t in range(TPB):
                    last = nc.tensor.transpose(ps[:, 5, S * g + P * t:S * g + P * (t + 1)], g_tok[:, t, g, :], ident[:])
            last.then_inc(g_tr, 1)
            pe.wait_ge(en_ready, 1)
            for t in range(TPB):
                last = nc.tensor.transpose(ps[:, 6, P * t:P * (t + 1)], en_h[:, P * t:P * (t + 1)], ident[:])
            last.then_inc(en_tr, 1)
            pe.wait_ge(consts, 2)
            pe.wait_ge(v_ready, B)
            pe.wait_ge(lo_ready, 2 * B)
            pe.wait_ge(am_ready, 1)
            pe.wait_ge(en_tok, 1)

            def exponents(b, u, turn, pair):
                n, q = NH // 2 * b + pair, pair % 2
                if pair == 0:
                    pe.wait_ge(heads_in[u], 8 * 16 * (turn + 1))
                wait_from(pe, decay_ready, n - 1)
                for j in range(2):
                    h = 2 * pair + j
                    bank = ps[:, 2 * q + j]
                    nc.tensor.matmul(bank[:, 0:S], a_rows[:, u, h, 0:P], m_rows[:, u, h, :], start=True, stop=False,
                                     skip_group_check=True)
                    nc.tensor.matmul(bank[:, S:S + P], a_rows[:, u, h, P:S], m_rows[:, u, h, P:S], start=False,
                                     stop=False, skip_group_check=True)
                    for k in (0, 2):
                        last = nc.tensor.matmul(bank[:, P * k:P * (k + 1)], ident_b[:], causal[:], start=False,
                                                stop=True, skip_group_check=True)
                last.then_inc(arg_ready, 1)

            def scores(b, u, pair):
                n = NH // 2 * b + pair
                for j in range(2):
                    h = 2 * pair + j
                    wait_from(pe, c_ready, 2 * n - 1 + j)
                    nc.tensor.matmul(ps[:, 4 + j, 0:S], ks[:, u, h, 0:P], qs[:, u, h, :], start=True, stop=True)
                    nc.tensor.matmul(ps[:, 4 + j, S:S + P], ks[:, u, h, P:S], qs[:, u, h, P:S], start=True,
                                     stop=True).then_inc(s_ready, 1)

            def heads(b, pair):
                n, side = NH // 2 * b + pair, pair // 2
                pe.wait_ge(c_lo, n + 1)
                if pair % 2 == 0:
                    wait_from(pe, h_read, 2 * b + side - 1)
                bank = ps[:, 6 + side, 0:TPB * (NH // 2) * (DH + 1)].rearrange("p (t h e) -> p t h e", t=TPB, h=NH // 2)
                for j in range(2):
                    h = 2 * pair + j
                    for t, blocks in ((0, ((0, 0),)), (1, ((1, 0), (2, 1)))):
                        terms = [(block, kt, a, g) for block, kt in blocks for a, g in ((0, 0), (0, 1), (1, 0))]
                        for k, (block, kt, a, g) in enumerate(terms):
                            last = nc.tensor.matmul(
                                bank[:, t, h % (NH // 2), :], c16[:, pair, a, j, P * block:P * (block + 1)],
                                v_ext[:, g, at(TPB * b + kt), h, 0:DH + 1].rearrange("p o e -> p (o e)"),
                                start=k == 0, stop=k == len(terms) - 1)
                last.then_inc(h_ready, 1)

            def attend(b, u, i, first=False, last=False):
                for pair in range(NH // 2):
                    ahead = (b, u, i, pair + 1) if pair < NH // 2 - 1 else None if last else (b + 1, 1 - u, i + u, 0)
                    if ahead:
                        exponents(*ahead)
                    if pair >= 2 or not first:
                        heads(b if pair >= 2 else b - 1, (pair - 2) % (NH // 2))
                    if ahead:
                        scores(ahead[0], ahead[1], ahead[3])

            exponents(0, 0, 0, 0)
            scores(0, 0, 0)
            attend(0, 0, 0, first=True)
            attend(1, 1, 0)
            with pe.Fori(1, B // 2 - 1) as i:
                for u in range(2):
                    attend(2 * i + u, u, i)
            attend(B - 2, 0, B // 2 - 1)
            attend(B - 1, 1, B // 2 - 1, last=True)
            for pair in (2, 3):
                heads(B - 1, pair)

            pe.wait_ge(rg_ready, 1)
            SPLIT = ((0, 0), (0, 1), (1, 0))

            def transpose_rows(bank, src):
                view = ps[:, bank, 0:D].bitcast(F16)
                for k in range(2 * C):
                    last = nc.tensor.transpose(view[:, P * k:P * (k + 1)], src[:, P * k:P * (k + 1)], ident_h[:])
                return last

            def logits(n, p):
                pe.wait_ge(row_copied, n + 1)
                terms = [(c, a, g) for c in range(C) for a, g in SPLIT]
                for k, (c, a, g) in enumerate(terms):
                    last = nc.tensor.matmul(ps[:, 6, at(E * n, E)], xt[:, p, D * a + P * c:D * a + P * (c + 1)],
                                            rg16[:, g, c, :], start=k == 0, stop=k == len(terms) - 1)
                last.then_inc(logits_done, 1)

            def row_turn(n, p, i):
                pe.wait_ge(xlo_ready, n + 1)
                wait_from(pe, row_copied, n - 1)
                transpose_rows(p, xr[:, at(n), 0:2 * D].rearrange("p o d -> p (o d)")).then_inc(row_tr, 1)
                if not isinstance(n, int) or n > 0:
                    logits(n - 1, 1 - p)

            stepped(pe, 2, TT, row_turn)
            logits(TT - 1, (TT - 1) % 2)
            pe.wait_ge(hot_ready, 1)
            pe.wait_ge(lg_read, 1)
            nc.tensor.matmul(ps[:, 6, 0:TT * E], earlier[:], hot_b[:].rearrange("p t e -> p (t e)"), start=True, stop=True)
            nc.tensor.matmul(ps[:, 6, TT * E:2 * TT * E], ones_b[:], hot_b[:].rearrange("p t e -> p (t e)"), start=True,
                             stop=True).then_inc(ranks_done, 1)

            def turn_x(n, src):
                wait_from(pe, xt_ready, n)
                transpose_rows(7, src).then_inc(x_tr, 1)

            def turn_own(n):
                turn_x(n, xr[:, at(n), 0:2 * D].rearrange("p o d -> p (o d)"))

            def turn_slots(k, u, i):
                pe.wait_ge(rows_in[u], 16 * i + 16)
                turn_x(TT + k, rows[:, u, 0:2 * D])

            def up(n, p, piece):
                pe.wait_ge(xt_ready, n + 1)
                wait_from(pe, hid_ready, n - 1)
                for m, done in ((0, up1), (1, up2)):
                    terms = [(c, a, g) for c in range(C) for a, g in SPLIT]
                    for k, (c, a, g) in enumerate(terms):
                        w = w16[:, at(piece + m), g, HID * c:HID * (c + 1)].rearrange("p o n -> p (o n)")
                        last = nc.tensor.matmul(ps[:, 2 * m + p], xt[:, p, D * a + P * c:D * a + P * (c + 1)], w,
                                                start=k == 0, stop=k == len(terms) - 1)
                    last.then_inc(done, 1)

            def down(n, p, piece):
                pe.wait_ge(hid_lo, n + 1)
                terms = [(c, a, g) for c in range(KH) for a, g in SPLIT]
                for k, (c, a, g) in enumerate(terms):
                    w = w16[:, at(piece + 2), g, D * c:D * (c + 1)].rearrange("p o n -> p (o n)")
                    last = nc.tensor.matmul(ps[:, 5, 0:D], hid_t[:, p, a, P * c:P * (c + 1)], w,
                                            start=k == 0, stop=k == len(terms) - 1)
                last.then_inc(down_done, 1)

            def turn_hid(n, p):
                pe.wait_ge(hid_ready, n + 1)
                wait_from(pe, hid_lo, n)
                for c in range(KH):
                    last = nc.tensor.transpose(ps[:, 4, P * c:P * (c + 1)], hid[:, p, P * c:P * (c + 1)], ident[:])
                last.then_inc(hid_tr, 1)

            def shared_step(n, p, half):
                up(n, p, 0)
                if not isinstance(n, int) or n < TT - 1:
                    turn_own(n + 1)
                else:
                    turn_slots(0, 0, 0)
                if not isinstance(n, int) or n > 0:
                    wait_from(pe, y_ready, n - 1)
                    down(n - 1, 1 - p, 0)
                turn_hid(n, p)

            pe.wait_ge(piece_lo, 3)
            pe.wait_ge(routed, 2)
            turn_own(0)
            for n in range(3):
                shared_step(n, n % 2, 0)
            looped(pe, 2, 3, TT - 1, shared_step)
            shared_step(TT - 1, 1, 0)

            expert_of = [pe.alloc_register(f"expert_of{u}") for u in range(4)]

            def load_expert(k, u):
                pe.reg_load(expert_of[u], tile_e[0:1, at(k)])

            def pieces_of(u):
                return 3 + 3 * pe.snap(expert_of[u], min_val=0, max_val=E - 1)

            def expert_step(k, u, i):
                first, last = (isinstance(k, int) and k == n for n in (0, NT - 1))
                own, before = pieces_of(u), None if first else pieces_of((u - 1) % 4)
                up(TT + k, u % 2, own)
                if not last:
                    load_expert(k + 1, (u + 1) % 4)
                    turn_slots(k + 1, (u + 1) % 4, i + (u + 1) // 4)
                if first:
                    pe.wait_ge(y_ready, TT - 1)
                    down(TT - 1, 1, 0)
                else:
                    if isinstance(k, int) and k == 1:
                        pe.wait_ge(y_ready, TT)
                    else:
                        pe.wait_ge(ye_ready, k - 1)
                    down(TT + k - 1, 1 - u % 2, before)
                turn_hid(TT + k, u % 2)

            load_expert(0, 0)
            pe.wait_ge(piece_lo, PIECES)
            for k in range(4):
                expert_step(k, k, 0)
            looped(pe, 4, 4, NT - 3, expert_step)
            for k in range(NT - 3, NT):
                expert_step(k, k % 4, k // 4)
            before = pieces_of((NT - 1) % 4)
            pe.wait_ge(ye_ready, NT - 1)
            down(TT + NT - 1, (NT - 1) % 2, before)


_INS = ['x', 'ctx_1024', 'g_xattn', 'g_ffn', 'L0_xattn_igate_w', 'L0_xattn_igate_b', 'L0_xattn_fgate_w',
        'L0_xattn_fgate_b', 'L0_xattn_ln_scale', 'L0_ffn_gate_w', 'L0_ffn_ew1', 'L0_ffn_ew2', 'L0_ffn_ew3',
        'L0_ffn_sw1', 'L0_ffn_sw2', 'L0_ffn_sw3']


def kernel(**inputs):
    import numpy as _np
    import concourse.bacc as _bacc
    from concourse import mybir as _mybir
    from concourse.bass_utils import run_bass_kernel_spmd as _run

    nc = _bacc.Bacc("TRN2", target_bir_lowering=False, num_devices=1)
    arrays, args = {}, []
    for name in _INS:
        a = _np.ascontiguousarray(inputs[name])
        arrays[f"in_{name}_dram"] = a
        args.append(nc.dram_tensor(f"in_{name}_dram", a.shape, _mybir.dt.from_np(a.dtype), kind="ExternalInput").ap())
    b, s, d = inputs['x'].shape
    args.append(nc.dram_tensor("out_0_dram", (b * s + P, d), _mybir.dt.float32, kind="ExternalOutput").ap())
    flamingo_block(nc, *args)
    r = _run(nc, [arrays], core_ids=[0])
    return r.results[0]["out_0_dram"][:b * s].reshape(b, s, d)
```

```python
from contextlib import ExitStack

import concourse.bass as bass
from concourse import mybir

F32 = mybir.dt.float32
F16 = mybir.dt.float16
BF16 = mybir.dt.bfloat16
I32 = mybir.dt.int32
U32 = mybir.dt.uint32
ALU = mybir.AluOpType
ACT = mybir.ActivationFunctionType
AX = mybir.AxisListType

P = 128
LN_EPS = 1e-5
DEN_EPS = 1e-6
MASKED = -1e30
W_SCALE = 64.0


def at(n, count=1):
    return bass.ds(n, count)


def wait_from(eng, sem, value):
    if isinstance(value, int) and value <= 0:
        return
    eng.wait_ge(sem, value)


class Steps:

    def __init__(self, eng, sem, base=0):
        self.eng, self.sem, self.base, self.n = eng, sem, base, 0

    def then(self, instruction):
        instruction.then_inc(self.sem, 1)
        self.n += 1
        self.eng.wait_ge(self.sem, self.base + self.n)


def stepped(eng, unroll, total, step):
    for u in range(unroll):
        step(u, u, 0)
    with eng.Fori(1, total // unroll) as i:
        for u in range(unroll):
            step(unroll * i + u, u, i)


def looped(eng, unroll, first, end, step):
    with eng.Fori(0, (end - first) // unroll) as i:
        for u in range(unroll):
            step(unroll * i + (first + u), (first + u) % unroll, i + (first + u) // unroll)


def within(b, lag, batches):
    return not isinstance(b, int) or 0 <= b - lag < batches


def flamingo_block(nc, x, ctx_in, g_xattn, g_ffn, igate_w, igate_b, fgate_w, fgate_b, ln_scale,
                   gate_w, ew1, ew2, ew3, sw1, sw2, sw3, out):
    B, S, D = x.shape
    NH = igate_w.shape[0]
    DH = D // NH
    VW = DH + 2
    E = gate_w.shape[1]
    HID = ew1.shape[2]
    TPB = S // P
    TT = B * TPB
    C = D // P
    HPC = NH // C
    BH = B * NH
    DONE = TPB * (B - 3)
    assert BH == P and DH == 32 and HID == 4 * P and TPB == 2
    QK_SCALE = DH ** -0.5
    KH = HID // P
    PIECE = C * HID
    PIECES = 3 * (E + 1)
    TOP = 2
    NT = (TOP * TT * P + E * (P - 1)) // P
    PADS = E + NT - TOP * TT
    ROW = 2 * D + 32

    es = ExitStack()
    with es:
        def sb(name, shape, dt, stack=es):
            return stack.enter_context(nc.sbuf_tensor(name, shape, dt))

        def sem(name):
            return es.enter_context(nc.semaphore(name))

        x_v = x.rearrange("b (t p) d -> p (b t) d", p=P)
        c_v = ctx_in.rearrange("b (t p) d -> p (b t) d", p=P)
        out_v = out[0:TT * P, :].rearrange("(t p) d -> p t d", p=P)
        qk = nc.dram_tensor("qk_split", [B, 2, 2, NH, DH, S], F16, kind="Internal").ap()
        slots = nc.dram_tensor("slots", [(NT + PADS) * P, ROW // 2], U32, kind="Internal").ap()
        am = nc.dram_tensor("gate_parts", [3, 2, BH, S], BF16, kind="Internal").ap()

        ident = sb("ident", [P, P], F32)
        ident_h = sb("ident_h", [P, P], F16)
        earlier = sb("earlier", [P, P], BF16)
        ones_b = sb("ones_b", [P, P], BF16)
        pad_row = sb("pad_row", [P, ROW // 2], U32)
        xs = sb("xs", [P, TT, D], F32)
        stage = sb("stage", [P, 2, PIECE], F32)
        half = sb("half", [P, TT], F32)
        small = sb("small", [P, 7, TT], F32)
        mean = sb("mean", [P, TT], F32)
        rstd = sb("rstd", [P, TT], F32)
        stats = sb("stats", [P, TT, 6], F32)
        gains = sb("gains", [P, 2], F32)
        gains_in = sb("gains_in", [P, 2], F32)
        ps = es.enter_context(nc.psum_tensor("ps", [P, 8, 512], F32))

        early = ExitStack()
        with early:
            ln_gain = sb("ln_gain", [P, D], F32, early)
            ident_b = sb("ident_b", [P, P], BF16, early)
            causal = sb("causal", [P, P], BF16, early)
            v_ext = sb("v_ext", [P, 2, TT, NH, VW], F16, early)
            gw_rows = sb("gw_rows", [2 * NH, 3 * D], F32, early)
            gw_sum = sb("gw_sum", [P, 2, C, 2 * NH], F32, early)
            gw = sb("gw", [P, 2, 2, C, 2 * NH], F16, early)
            gw_tmp = sb("gw_tmp", [P, C, 2 * NH], F32, early)
            split = sb("split", [P, 4, 2, 2, C, S], F16, early)
            g_tok = sb("g_tok", [P, TPB, 2, BH], F32, early)
            bias = sb("bias", [P, 2, NH], F32, early)
            ones = sb("ones", [P, S], F32, early)
            zf = sb("zf", [P, S], F32, early)
            zt = sb("zt", [P, S], F32, early)
            lf = sb("lf", [P, S], F32, early)
            cs = sb("cs", [P, S], F32, early)
            am32 = sb("am32", [P, 2, S], F32, early)
            am_r = sb("am_r", [P, 2, S], F32, early)
            am_p = sb("am_p", [P, 3, 2, S], BF16, early)
            nd = sb("nd", [P, S], F32, early)
            en_h = sb("en_h", [P, S], F32, early)
            en = sb("en", [P, TPB, BH], F32, early)
            ks = sb("ks", [3 * DH, 2, NH, S], F16, early)
            qs = sb("qs", [3 * DH, 2, NH, S], F16, early)
            a_rows = sb("a_rows", [6, 2, NH, S], BF16, early)
            m_rows = sb("m_rows", [6, 2, NH, S], BF16, early)
            loading = ExitStack()
            with loading:
                c_raw = sb("c_raw", [P, 8, TPB, D], F32, loading)
                qn = sb("qn", [P, 2, TPB, D], F32, loading)
            decay = sb("decay", [P, 2, 2, 3 * P], F32, early)
            cmat = sb("cmat", [P, 2, 2, 3 * P], F32, early)
            c16 = sb("c16", [P, NH // 2, 2, 2, 3 * P], F16, early)
            den = sb("den", [P, 2, 2, TPB, NH // 2], F32, early)
            h_bn = sb("h_bn", [P, 2, TPB, 6], F32, early)
            h_mv = sb("h_mv", [P, 2, TPB, 2], F32, early)
            h_scale = sb("h_scale", [P, 2, TPB], F32, early)
            eps = sb("eps", [P, TPB], F32, early)
            hbuf = sb("hbuf", [P, TT, D], F32, early)

        w16 = sb("w16", [P, PIECES, 2, PIECE], F16)
        xr_w = sb("xr", [P, TT, ROW // 2], U32)
        xr = xr_w[:].bitcast(F16)
        xt = sb("xt", [P, 2, 2 * D], F16)
        slot_i = sb("slot_i", [P, TOP, TT], U32)
        tile_e = sb("tile_e", [P, NT], I32)
        pad_slot = sb("pad_slot", [P, PADS], U32)
        normal_rows = ExitStack()
        with normal_rows:
            xn = sb("xn", [P, 4, D], F32, normal_rows)
        act_g = sb("act_g", [P, HID], F32)
        hid = sb("hid", [P, HID], F32)
        hid_t = sb("hid_t", [P, 2, HID], F16)
        y = sb("y", [P, 2, D], F32)
        row_t = [xt[:, 0], xt[:, 1], hid_t[:, 0], hid_t[:, 1]]
        routing = ExitStack()
        with routing:
            rg = sb("rg", [P, C, E], F32, routing)
            rg16 = sb("rg16", [P, 2, C, E], F16, routing)
            lg = sb("lg", [P, TT, E], F32, routing)
            hot = sb("hot", [P, TOP, TT, E], F32, routing)
            hot_b = sb("hot_b", [P, TT, E], BF16, routing)
            pos = sb("pos", [P, TT, E], F32, routing)
            cum = sb("cum", [P, TT, E], F32, routing)
            top = sb("top", [P, 8, TT], F32, routing)
            slot_f = sb("slot_f", [P, TOP, TT], F32, routing)
            per_e = sb("per_e", [P, 4, E], F32, routing)
            past = sb("past", [P, NT, E], F32, routing)
            tile_f = sb("tile_f", [P, NT], F32, routing)
            count_i = sb("count_i", [P, NT], I32, routing)
            count_f = sb("count_f", [P, NT], F32, routing)
            rev = sb("rev", [P, E], F32, routing)
            thresh = sb("thresh", [P, TT], F32, routing)
            ones_t = sb("ones_t", [P, TT], F32, routing)
            own_f = sb("own_f", [P, 1], F32, routing)
            spare_f = sb("spare_f", [P, PADS], F32, routing)
            pad_f = sb("pad_f", [P, 2, PADS], F32, routing)
            pad_end = sb("pad_end", [P, PADS], F32, routing)
            tmp = past[:, 0:TT]
            fill = lg[:].rearrange("p t e -> p (t e)").rearrange("p (e t) -> p e t", e=E)
        rows_w = sb("rows", [P, 4, ROW // 2], U32)
        rows = rows_w[:].bitcast(F16)
        meta = xr_w[:, :, D:ROW // 2].bitcast(F32)

        gates_ps = ps[:, 4, :].rearrange("p (t g n) -> p t g n", t=TPB, g=2)

        x_in = [sem(f"x_in{u}") for u in range(4)]
        c_in = [sem(f"c_in{u}") for u in range(8)]
        gw_in, vec_in = sem("gw_in"), sem("vec_in")
        consts, pool_step, half_set = sem("consts"), sem("pool_step"), sem("half_set")
        gw_tr, gw_ready = sem("gw_tr"), sem("gw_ready")
        var_ready, rstd_ready = sem("var_ready"), sem("rstd_ready")
        qn_ready, q_tr, k_tr, hi_ready, lo_ready = (sem(n) for n in ("qn_ready", "q_tr", "k_tr", "hi_ready", "lo_ready"))
        split_out = [sem(f"split_out{u}") for u in range(4)]
        gates_done, v_ready = sem("gates_done"), sem("v_ready")
        g_copied, g_tr, exp_ready, ln_ready, nabs_ready = (
            sem(n) for n in ("g_copied", "g_tr", "exp_ready", "ln_ready", "nabs_ready"))
        nd_ready, en_ready, en_tr, en_tok = (sem(n) for n in ("nd_ready", "en_ready", "en_tr", "en_tok"))
        am_ready, am_out = sem("am_ready"), sem("am_out")
        dve_step, x_stats_done, division, residual_added = (
            sem(n) for n in ("dve_step", "x_stats_done", "division", "residual_added"))
        heads_in = [sem(f"heads_in{u}") for u in range(2)]
        arg_ready, s_ready, decay_ready, c_ready, c_hi, c_lo, h_ready, h_read = (
            sem(n) for n in ("arg_ready", "s_ready", "decay_ready", "c_ready", "c_hi", "c_lo", "h_ready", "h_read"))
        gain_set, v_hi = sem("gain_set"), sem("v_hi")
        h_stats, h_mv_ready, h_var, h_rstd, h_gained, x1_stats = (
            sem(n) for n in ("h_stats", "h_mv_ready", "h_var", "h_rstd", "h_gained", "x1_stats"))
        tanh_ready = sem("tanh_ready")
        pad_set, pad_out = sem("pad_set"), sem("pad_out")
        rg_in, rg_ready, numbers = sem("rg_in"), sem("rg_ready"), sem("numbers")
        xn_ready, xhi_ready, xlo_ready, row_tr, row_copied, logits_done = (
            sem(n) for n in ("xn_ready", "xhi_ready", "xlo_ready", "row_tr", "row_copied", "logits_done"))
        lg_read, gap_ready, gap_exp, hot_ready, ranks_done = (
            sem(n) for n in ("lg_read", "gap_ready", "gap_exp", "hot_ready", "ranks_done"))
        routed, meta_set, scattered = sem("routed"), sem("meta_set"), sem("scattered")
        stage_in = [sem(f"stage_in{u}") for u in range(2)]
        rows_in = [sem(f"rows_in{u}") for u in range(4)]
        piece_hi, piece_lo = sem("piece_hi"), sem("piece_lo")
        x_tr, xt_ready, up1, up2, silu, hid_ready, hid_tr, hid_hi, hid_lo, down_done = (
            sem(n) for n in ("x_tr", "xt_ready", "up1", "up2", "silu", "hid_ready", "hid_tr", "hid_hi", "hid_lo",
                             "down_done"))
        y_ready, y_out = sem("y_ready"), [sem(f"y_out{u}") for u in range(2)]
        ye_ready, add_turn, added = sem("ye_ready"), sem("add_turn"), sem("added")

        block = es.enter_context(nc.Block())

        @block.sync
        def _(sp):
            def load_x(b, u, i):
                wait_from(sp, x_in[u], 16 * i)
                sp.dma_start(xs[:, at(TPB * b, TPB)], x_v[:, at(TPB * b, TPB)]).then_inc(x_in[u], 16)

            def load_ctx(b, u, i):
                wait_from(sp, k_tr, b - 7)
                wait_from(sp, v_ready, b - 7)
                sp.dma_start(c_raw[:, u], c_v[:, at(TPB * b, TPB)]).then_inc(c_in[u], 16)

            stepped(sp, 4, B, load_x)
            stepped(sp, 8, B, load_ctx)

            for u in range(4):
                sp.wait_ge(split_out[u], 16 * (B // 4))

            def load_qk(b, u):
                for dst, which, parts in ((qs, 0, (0, 1, 0)), (ks, 1, (0, 0, 1))):
                    for r, part in enumerate(parts):
                        sp.dma_start(dst[DH * r:DH * (r + 1), u],
                                     qk[at(b), which, part].rearrange("o h d s -> d (o h) s")).then_inc(heads_in[u], 16)

            def load_gates(b, u):
                sp.dma_start(m_rows[0:3, u], am[:, 0, at(NH * b, NH), :]).then_inc(heads_in[u], 16)
                sp.dma_start(a_rows[3:6, u], am[:, 1, at(NH * b, NH), :]).then_inc(heads_in[u], 16)

            def load_heads(b, u, i):
                sp.wait_ge(s_ready, NH * (b - 1))
                load_qk(b, u)
                load_gates(b, u)

            for b in range(2):
                load_qk(b, b)
            sp.wait_ge(am_ready, 1)
            sp.dma_start(am.rearrange("a k n s -> n a k s"), am_p[:]).then_inc(am_out, 16)
            sp.wait_ge(am_out, 16)
            for b in range(2):
                load_gates(b, b)
            looped(sp, 2, 2, B, load_heads)

            def load_piece(src, slot):
                sp.dma_start(stage[:, slot], src).then_inc(stage_in[slot], 16)

            def expert_piece(e, m):
                w, chunks = ((ew1, C), (ew2, C), (ew3, KH))[m]
                return w[at(e)].rearrange("e (c p) n -> p (e c) n", c=chunks)

            shared_pieces = [w.rearrange("(c p) n -> p c n", p=P) for w in (sw1, sw2, sw3)]
            for k in range(2):
                load_piece(shared_pieces[k], k)
            sp.wait_ge(h_ready, NH // 2 * B)
            sp.wait_ge(residual_added, B)
            for c in range(C):
                sp.dma_start(rg[:, c], gate_w[P * c:P * (c + 1), :]).then_inc(rg_in, 16)
            sp.wait_ge(piece_lo, 1)
            load_piece(shared_pieces[2], 0)
            for k in (3, 4):
                sp.wait_ge(piece_lo, k - 1)
                load_piece(expert_piece(0, k - 3), k % 2)

            def store_shared(n, p):
                sp.wait_ge(y_ready, n + 1)
                sp.dma_start(out_v[:, at(n)], y[:, p:p + 1]).then_inc(y_out[p], 16)

            def shared_turn(n, u, e, m):
                store_shared(n - 1, (u - 1) % 2)
                sp.wait_ge(piece_lo, n + 3)
                load_piece(expert_piece(e, m), u % 2)

            with sp.Fori(0, 3) as i:
                for u in range(6):
                    shared_turn(6 * i + (u + 1), u + 1, 2 * i + (u + 2) // 3, (u + 2) % 3)
            for n in range(19, PIECES - 4):
                shared_turn(n, n, (n + 1) // 3, (n + 1) % 3)
            for n in range(PIECES - 4, TT - 1):
                store_shared(n - 1, (n - 1) % 2)

            sp.wait_ge(scattered, 16 * (TOP * TT + PADS))

            def load_rows(k, u, i):
                wait_from(sp, added, 16 * (k - 3))
                sp.dma_start(rows_w[:, u], slots[at(P * k, P), :]).then_inc(rows_in[u], 16)

            for k in range(4):
                load_rows(k, k, 0)
            for n in (TT - 2, TT - 1):
                store_shared(n, n % 2)
            looped(sp, 4, 4, NT - 3, load_rows)
            for k in range(NT - 3, NT):
                load_rows(k, k % 4, k // 4)
            sp.wait_ge(added, 16 * NT)

        @block.gpsimd
        def _(pool):
            order = Steps(pool, pool_step)
            order.then(nc.gpsimd.memset(ident[:], 0.0))
            order.then(nc.gpsimd.affine_select(out=ident[:], in_=ident[:], compare_op=ALU.not_equal, fill=1.0,
                                               base=0, pattern=[[-1, P]], channel_multiplier=1))
            nc.gpsimd.tensor_copy(ident_h[:], ident[:])
            order.then(nc.gpsimd.memset(causal[:], 0.0))
            order.then(nc.gpsimd.affine_select(out=causal[:], in_=causal[:], compare_op=ALU.is_ge, fill=MASKED,
                                               base=0, pattern=[[1, P]], channel_multiplier=-1))
            nc.gpsimd.memset(ones[:], 1.0)
            nc.gpsimd.tensor_copy(ident_b[:], ident[:]).then_inc(consts, 1)
            order.then(nc.gpsimd.memset(earlier[:], 1.0))
            order.then(nc.gpsimd.affine_select(out=earlier[:], in_=earlier[:], compare_op=ALU.is_ge, fill=0.0,
                                               base=-1, pattern=[[1, P]], channel_multiplier=-1))
            nc.gpsimd.memset(ones_b[:], 1.0)
            order.then(nc.gpsimd.memset(pad_row[:], 0))
            nc.gpsimd.iota(pad_row[:, D + E:D + E + 1].bitcast(I32), pattern=[[0, 1]], base=TT * P,
                           channel_multiplier=1).then_inc(pad_set, 1)
            nc.gpsimd.memset(eps[:], LN_EPS)
            nc.gpsimd.memset(half[:], -0.5).then_inc(half_set, 1)
            pool.wait_ge(half_set, 1)
            nc.gpsimd.memset(a_rows[:], 1.0)
            nc.gpsimd.memset(m_rows[:], 1.0)
            nc.gpsimd.memset(v_ext[:, 0, :, :, DH:VW], 1.0)
            nc.gpsimd.memset(v_ext[:, 1, :, :, DH:VW], 0.0).then_inc(consts, 1)

            def reciprocal_root(n, tiles):
                pool.wait_ge(var_ready, n)
                nc.gpsimd.tensor_tensor(rstd[:, tiles], small[:, 6, tiles], half[:, tiles], ALU.pow).then_inc(rstd_ready, 1)

            reciprocal_root(1, slice(0, TT // 2))
            reciprocal_root(2, slice(TT // 2, TT))

            def values(b, u, i):
                v = c_raw[:, u].rearrange("p t (h d) -> p t h d", h=NH)
                v_high, v_low = (v_ext[:, k, at(TPB * b, TPB), :, 0:DH] for k in range(2))
                pool.wait_ge(v_hi, b + 1)
                nc.gpsimd.tensor_tensor(v_low, v, v_high, ALU.subtract).then_inc(v_ready, 1)

            stepped(pool, 8, B, values)
            pool.wait_ge(pad_set, 1)
            pool.dma_start(out[TT * P:TT * P + P, :], pad_row[:, 0:D].bitcast(F32)).then_inc(pad_out, 16)

            def mixed_low(b, u, i):
                for pair in range(NH // 2):
                    if within(b, 0, B):
                        pool.wait_ge(c_hi, NH // 2 * b + pair + 1)
                        nc.gpsimd.tensor_tensor(c16[:, pair, 1], cmat[:, pair % 2], c16[:, pair, 0],
                                                ALU.subtract).then_inc(c_lo, 1)
                    if pair == 1 and within(b, 2, B):
                        head_scale(b - 2, u)

            def head_scale(b, slot):
                pool.wait_ge(h_mv_ready, b + 1)
                nc.gpsimd.tensor_tensor(h_scale[:, slot], h_mv[:, slot, :, 1], eps[:], ALU.add).then_inc(h_var, 1)
                pool.wait_ge(h_var, b + 1)
                nc.gpsimd.tensor_tensor(h_scale[:, slot], h_scale[:, slot], half[:, 0:TPB], ALU.pow).then_inc(h_rstd, 1)

            for b in range(2):
                mixed_low(b, b, 0)
            looped(pool, 2, 2, B, mixed_low)
            mixed_low(B, 0, 0)
            reciprocal_root(3, slice(0, DONE))
            mixed_low(B + 1, 1, 0)
            pool.wait_ge(h_ready, NH // 2 * B)
            pool.wait_ge(residual_added, B)
            reciprocal_root(4, slice(DONE, TT))

            def number(dst, columns, pattern, base):
                order.then(nc.gpsimd.iota(count_i[:, 0:columns], pattern=pattern, base=base, channel_multiplier=0))
                order.then(nc.gpsimd.tensor_copy(dst, count_i[:, 0:columns]))

            number(rev[:], E, [[-1, E]], E)
            number(thresh[:], TT, [[P, TT]], 0)
            number(count_f[:], NT, [[1, NT]], 0)
            order.then(nc.gpsimd.iota(count_i[:, 0:1], pattern=[[0, 1]], base=0, channel_multiplier=1))
            order.then(nc.gpsimd.tensor_copy(own_f[:], count_i[:, 0:1]))
            order.then(nc.gpsimd.iota(count_i[:, 0:PADS], pattern=[[P, PADS]], base=NT * P, channel_multiplier=1))
            order.then(nc.gpsimd.tensor_copy(spare_f[:], count_i[:, 0:PADS]))
            nc.gpsimd.memset(pad_end[:], float(NT * P))
            nc.gpsimd.memset(ones_t[:], 1.0).then_inc(numbers, 1)
            order.then(nc.gpsimd.memset(meta, 0.0))
            nc.gpsimd.iota(xr_w[:, :, D + E:D + E + 1].bitcast(I32), pattern=[[P, TT], [0, 1]], base=0,
                           channel_multiplier=1).then_inc(meta_set, 1)

            pool.wait_ge(routed, 1)
            pool.wait_ge(meta_set, 2)
            pool.wait_ge(pad_out, 16)
            for k in range(TOP):
                for t in range(TT):
                    nc.gpsimd.indirect_dma_start(
                        out=slots, out_offset=bass.IndirectOffsetOnAxis(ap=slot_i[:, k, t:t + 1], axis=0),
                        in_=xr_w[:, t, :], in_offset=None).then_inc(scattered, 16)
            pool.wait_ge(routed, 3)
            for c in range(PADS):
                nc.gpsimd.indirect_dma_start(
                    out=slots, out_offset=bass.IndirectOffsetOnAxis(ap=pad_slot[:, c:c + 1], axis=0),
                    in_=pad_row[:], in_offset=None).then_inc(scattered, 16)

            for p in range(2):
                pool.wait_ge(y_out[p], 16 * TT // 2)

            def add_rows(k, u, i):
                pool.wait_ge(ye_ready, k + 1)
                wait_from(pool, added, 16 * k)
                pool.sem_inc(add_turn, 1)
                nc.gpsimd.indirect_dma_start(
                    out=out, out_offset=bass.IndirectOffsetOnAxis(
                        ap=rows_w[:, u, D + E:D + E + 1], axis=0),
                    in_=y[:, u % 2], in_offset=None, compute_op=ALU.add).then_inc(added, 16)

            for k in range(4):
                add_rows(k, k, 0)
            looped(pool, 4, 4, NT - 3, add_rows)
            for k in range(NT - 3, NT):
                add_rows(k, k % 4, k // 4)

        @block.scalar
        def _(act):
            act.dma_start(gw_rows[0:NH, :], igate_w).then_inc(gw_in, 16)
            act.dma_start(gw_rows[NH:2 * NH, :], fgate_w).then_inc(gw_in, 16)
            act.dma_start(gains_in[:, 0:1], g_xattn.unsqueeze(0).partition_broadcast(P)).then_inc(vec_in, 16)
            act.dma_start(gains_in[:, 1:2], g_ffn.unsqueeze(0).partition_broadcast(P)).then_inc(vec_in, 16)
            act.dma_start(ln_gain[:], ln_scale.unsqueeze(0).partition_broadcast(P)).then_inc(vec_in, 16)
            act.dma_start(bias[:, 0, :], igate_b.unsqueeze(0).partition_broadcast(P)).then_inc(vec_in, 16)
            act.dma_start(bias[:, 1, :], fgate_b.unsqueeze(0).partition_broadcast(P)).then_inc(vec_in, 16)
            act.wait_ge(vec_in, 16 * 5)
            nc.scalar.activation(gains[:], gains_in[:], ACT.Tanh).then_inc(tanh_ready, 1)

            def store_split(b, u):
                act.wait_ge(lo_ready, 2 * b + 2)
                act.dma_start(qk[at(b)].rearrange("o w l (c g) d s -> (g d) (o w l) c s", c=C),
                              split[:, u].rearrange("p w l c s -> p (w l) c s")).then_inc(split_out[u], 16)

            def high(b, u, i):
                p = u % 2
                wait_from(act, split_out[u % 4], 16 * (2 * i + u // 4))
                wait_from(act, gates_done, b - 3)
                act.wait_ge(q_tr, b + 1)
                nc.scalar.activation(split[:, u % 4, 0, 0], ps[:, p], ACT.Copy).then_inc(hi_ready, 1)
                act.wait_ge(k_tr, b + 1)
                nc.scalar.activation(split[:, u % 4, 1, 0], ps[:, 2 + p], ACT.Copy).then_inc(hi_ready, 1)
                act.wait_ge(c_in[u], 16 * i + 16)
                nc.scalar.activation(v_ext[:, 0, at(TPB * b, TPB), :, 0:DH],
                                     c_raw[:, u].rearrange("p t (h d) -> p t h d", h=NH), ACT.Copy).then_inc(v_hi, 1)
                if not isinstance(b, int) or b > 0:
                    store_split(b - 1, (u - 1) % 4)

            stepped(act, 8, B, high)
            store_split(B - 1, 3)

            act.wait_ge(nabs_ready, 1)
            nc.scalar.activation(zt[:], zt[:], ACT.Exp).then_inc(exp_ready, 1)
            act.wait_ge(exp_ready, 1)
            nc.scalar.activation(zt[:], zt[:], ACT.Ln, bias=1.0).then_inc(ln_ready, 1)
            act.wait_ge(nd_ready, 1)
            nc.scalar.activation(en_h[:], nd[:], ACT.Exp, scale=-1.0).then_inc(en_ready, 1)

            def decays(n, q):
                act.wait_ge(arg_ready, n + 1)
                wait_from(act, c_ready, 2 * (n - 1))
                nc.scalar.activation(decay[:, q], ps[:, 2 * q:2 * q + 2, 0:3 * P], ACT.Exp).then_inc(decay_ready, 1)

            def mixed_high(n, pair):
                act.wait_ge(c_ready, 2 * n + 2)
                wait_from(act, h_ready, n - 3)
                nc.scalar.activation(c16[:, pair, 0], cmat[:, pair % 2], ACT.Copy).then_inc(c_hi, 1)

            def decays_and_high(b, u, i):
                for pair in range(NH // 2):
                    n = NH // 2 * b + pair
                    decays(n, pair % 2)
                    if within(b, 0 if pair else 1, B):
                        mixed_high(n - 1, (pair - 1) % (NH // 2))

            for b in range(2):
                decays_and_high(b, b, 0)
            looped(act, 2, 2, B, decays_and_high)
            mixed_high(NH // 2 * B - 1, NH // 2 - 1)

            def piece_high(k, slot, turn):
                act.wait_ge(stage_in[slot], 16 * turn + 16)
                nc.scalar.activation(w16[:, at(k), 0].rearrange("p o n -> p (o n)"), stage[:, slot], ACT.Copy,
                                     scale=W_SCALE).then_inc(piece_hi, 1)

            def copy_rows(n, u):
                act.wait_ge(row_tr, n + 1)
                wait_from(act, logits_done, n - 3)
                nc.scalar.activation(row_t[u % 4], ps[:, u % 4, 0:D].bitcast(F16), ACT.Copy).then_inc(row_copied, 1)

            def row_high(n, u, i):
                act.wait_ge(xn_ready, n + 1)
                nc.scalar.activation(xr[:, at(n), 0:D].rearrange("p o d -> p (o d)"), xn[:, u % 4],
                                     ACT.Copy).then_inc(xhi_ready, 1)
                if not isinstance(n, int) or n > 2:
                    copy_rows(n - 3, (u - 3) % 4)
                if isinstance(n, int) and n == 7:
                    piece_high(2, 0, 1)

            act.wait_ge(residual_added, B)
            for k in range(2):
                piece_high(k, k, 0)
            stepped(act, 8, TT, row_high)
            for n in range(TT - 3, TT):
                copy_rows(n, n % 4)
            act.wait_ge(logits_done, TT)

            def copy_x(n, p):
                act.wait_ge(x_tr, n + 1)
                wait_from(act, up2, n - 1)
                nc.scalar.activation(xt[:, p], ps[:, 7, 0:D].bitcast(F16), ACT.Copy).then_inc(xt_ready, 1)

            def gate_silu(n, p):
                act.wait_ge(up1, n + 1)
                wait_from(act, hid_ready, n)
                nc.scalar.activation(act_g[:], ps[:, p], ACT.Silu, scale=1.0 / W_SCALE).then_inc(silu, 1)

            def hid_high(n, p):
                act.wait_ge(hid_tr, n + 1)
                wait_from(act, down_done, n)
                nc.scalar.activation(hid_t[:, 0], ps[:, 4], ACT.Copy).then_inc(hid_hi, 1)

            def expert_y(k, u, i):
                e = act.value_load(tile_e[0:1, at(k)], min_val=0, max_val=E - 1)
                act.wait_ge(down_done, TT + k + 1)
                act.wait_ge(rows_in[u], 16 * i + 16)
                if isinstance(k, int) and k < 2:
                    act.wait_ge(y_out[k], 16 * (TT // 2))
                wait_from(act, added, 16 * (k - 1))
                nc.scalar.activation(y[:, u % 2], ps[:, 5, 0:D], ACT.Copy,
                                     scale=rows_w[:, u, D:D + E].bitcast(F32)[:, at(e)]).then_inc(ye_ready, 1)

            def shared_step(n, p, half, with_piece=True):
                gate_silu(n, p)
                copy_x(n + 1, 1 - p)
                hid_high(n, p)
                if with_piece:
                    piece_high(n + 2, p, half + 1)

            copy_x(0, 0)
            gate_silu(0, 0)
            copy_x(1, 1)
            act.wait_ge(gap_ready, 1)
            nc.scalar.activation(top[:, 4], top[:, 3], ACT.Exp, scale=1.0 / W_SCALE).then_inc(gap_exp, 1)
            hid_high(0, 0)
            shared_step(1, 1, 0)
            shared_step(2, 0, 1)
            looped(act, 2, 3, PIECES - 2, shared_step)
            looped(act, 2, PIECES - 2, TT - 1, lambda n, p, half: shared_step(n, p, half, False))
            shared_step(TT - 1, 1, 0, False)

            def expert_step(k, u, i, last=False):
                gate_silu(TT + k, u % 2)
                if not last:
                    copy_x(TT + k + 1, 1 - u % 2)
                if not isinstance(k, int) or k > 0:
                    expert_y(k - 1, (u - 1) % 4, i if u else i - 1)
                hid_high(TT + k, u % 2)

            for k in range(4):
                expert_step(k, k, 0)
            looped(act, 4, 4, NT - 3, expert_step)
            for k in range(NT - 3, NT):
                expert_step(k, k % 4, k // 4, k == NT - 1)
            expert_y(NT - 1, (NT - 1) % 4, (NT - 1) // 4)

        @block.vector
        def _(dve):
            order = Steps(dve, dve_step)
            def layer_stats(tiles):
                me, mo, ve, vo = (stats[:, tiles, k] for k in (1, 4, 2, 5))
                s = small[:, :, tiles]
                nc.vector.tensor_tensor(s[:, 0], me, mo, ALU.add)
                nc.vector.tensor_tensor(s[:, 1], me, mo, ALU.subtract)
                order.then(nc.vector.tensor_tensor(s[:, 2], ve, vo, ALU.add))
                nc.vector.tensor_scalar(mean[:, tiles], s[:, 0], 0.5, None, ALU.mult)
                order.then(nc.vector.scalar_tensor_tensor(s[:, 3], s[:, 1], 0.25, s[:, 1], ALU.mult, ALU.mult))
                order.then(nc.vector.scalar_tensor_tensor(s[:, 4], s[:, 2], 1.0 / D, s[:, 3], ALU.mult, ALU.add))
                nc.vector.tensor_scalar(s[:, 6], s[:, 4], LN_EPS, None, ALU.add).then_inc(var_ready, 1)

            def gate_weights():
                dve.wait_ge(gw_tr, 1)
                wt = ps[:, 5, 0:6 * 2 * NH].rearrange("p (k n) -> p k n", k=6)
                nc.vector.tensor_scalar(gw_sum[:, 0], wt[:, 0:2], W_SCALE, None, ALU.mult)
                order.then(nc.vector.tensor_scalar(gw_tmp[:], wt[:, 2:4], W_SCALE, None, ALU.mult))
                order.then(nc.vector.scalar_tensor_tensor(gw_sum[:, 1], wt[:, 4:6], W_SCALE, gw_tmp[:], ALU.mult,
                                                          ALU.add))
                order.then(nc.vector.tensor_copy(gw[:, :, 0], gw_sum[:]))
                nc.vector.tensor_tensor(gw[:, :, 1], gw_sum[:], gw[:, :, 0], ALU.subtract).then_inc(gw_ready, 1)

            def x_stats(b, u, i):
                dve.wait_ge(x_in[u], 16 * i + 16)
                for t in range(TPB):
                    last = nc.vector.bn_stats(stats[:, at(TPB * b + t)], xs[:, at(TPB * b + t)])
                last.then_inc(x_stats_done, 1)

            for first, end in ((0, B // 2), (B // 2, B)):
                looped(dve, 4, first, end, x_stats)
                dve.wait_ge(x_stats_done, end)
                layer_stats(slice(TPB * first, TPB * end))
            gate_weights()
            dve.wait_ge(rstd_ready, 1)

            def queries(b, u, i):
                p = u % 2
                wait_from(dve, q_tr, b - 1)
                for t in range(TPB):
                    n = TPB * b + t
                    last = nc.vector.tensor_scalar(qn[:, p, t], xs[:, at(n)].rearrange("p o d -> p (o d)"),
                                                   mean[:, at(n)], rstd[:, at(n)], ALU.subtract, ALU.mult)
                last.then_inc(qn_ready, 1)

            def low(b, u, i):
                p = u % 2
                for w in range(2):
                    dve.wait_ge(hi_ready, 2 * b + w + 1)
                    nc.vector.tensor_tensor(split[:, u, w, 1].rearrange("p c s -> p (c s)"), ps[:, 2 * w + p],
                                            split[:, u, w, 0].rearrange("p c s -> p (c s)"),
                                            ALU.subtract).then_inc(lo_ready, 1)

            def queries_and_low(b, u, i):
                queries(b + 1, u + 1, i)
                low(b, u, i)

            queries(0, 0, 0)
            for b in range(4):
                queries_and_low(b, b, 0)
            dve.wait_ge(rstd_ready, 2)
            looped(dve, 4, 4, B - 4, queries_and_low)
            for b in range(B - 4, B - 1):
                queries_and_low(b, b % 4, b // 4)
            low(B - 1, 3, B // 4 - 1)

            dve.wait_ge(gates_done, B)
            dve.wait_ge(vec_in, 16 * 5)
            for g in range(2):
                for t in range(TPB):
                    last = nc.vector.scalar_tensor_tensor(
                        g_tok[:, t, g].rearrange("p (b h) -> p b h", h=NH),
                        gates_ps[:, t, g].rearrange("p (b h) -> p b h", h=NH), 1.0 / W_SCALE,
                        bias[:, g].unsqueeze(1).broadcast_to([P, B, NH]), ALU.mult, ALU.add)
            last.then_inc(g_copied, 1)
            dve.wait_ge(g_tr, 1)
            ig, fg = ps[:, 5, 0:S], ps[:, 5, S:2 * S]
            order.then(nc.vector.tensor_copy(zf[:], fg))
            order.then(nc.vector.scalar_tensor_tensor(zt[:], zf[:], -1.0, zf[:], ALU.mult, ALU.min))
            nc.vector.tensor_scalar(zf[:], zf[:], 0.0, None, ALU.min).then_inc(nabs_ready, 1)
            dve.wait_ge(ln_ready, 1)
            order.then(nc.vector.tensor_tensor(lf[:], zf[:], zt[:], ALU.subtract))
            order.then(nc.vector.tensor_tensor_scan(cs[:], ones[:], lf[:], 0.0, ALU.mult, ALU.add))
            order.then(nc.vector.tensor_tensor(am32[:, 1], ig, cs[:], ALU.subtract))
            order.then(nc.vector.tensor_tensor_scan(lf[:], am32[:, 1], am32[:, 1], -3e38, ALU.max, ALU.max))
            order.then(nc.vector.tensor_scalar(am32[:, 0], lf[:], -1.0, None, ALU.mult))
            order.then(nc.vector.tensor_copy(am_p[:, 0], am32[:]))
            order.then(nc.vector.tensor_tensor(am_r[:], am32[:], am_p[:, 0], ALU.subtract))
            order.then(nc.vector.tensor_copy(am_p[:, 1], am_r[:]))
            order.then(nc.vector.tensor_tensor(am32[:], am_r[:], am_p[:, 1], ALU.subtract))
            nc.vector.tensor_copy(am_p[:, 2], am32[:]).then_inc(am_ready, 1)
            nc.vector.tensor_tensor(nd[:], cs[:], lf[:], ALU.add).then_inc(nd_ready, 1)
            dve.wait_ge(en_tr, 1)
            nc.vector.tensor_scalar(en[:].rearrange("p t n -> p (t n)"), ps[:, 6, 0:S], DEN_EPS, None,
                                    ALU.add).then_inc(en_tok, 1)
            dve.wait_ge(en_tok, 1)

            dve.wait_ge(tanh_ready, 1)
            order.then(nc.vector.tensor_scalar(gains[:, 1:2], gains[:, 1:2], W_SCALE ** -2, None, ALU.mult))
            nc.vector.tensor_scalar(ln_gain[:], ln_gain[:], gains[:, 0:1], None, ALU.mult).then_inc(gain_set, 1)
            dve.wait_ge(gain_set, 1)

            def mix(n, q, j):
                if j == 0:
                    dve.wait_ge(decay_ready, n + 1)
                    wait_from(dve, c_lo, n - 1)
                dve.wait_ge(s_ready, 2 * n + j + 1)
                nc.vector.scalar_tensor_tensor(cmat[:, q, j], ps[:, 4 + j, 0:3 * P], QK_SCALE, decay[:, q, j],
                                               ALU.mult, ALU.mult).then_inc(c_ready, 1)

            def divide(b, side, part):
                m = 2 * b + side
                h_ps = ps[:, 6 + side, 0:TPB * (NH // 2) * (DH + 1)].rearrange("p (t h e) -> p t h e", t=TPB, h=NH // 2)
                if part == 0:
                    dve.wait_ge(h_ready, 2 * (m + 1))
                    nc.vector.tensor_copy(den[:, side, 0], h_ps[:, :, :, DH]).then_inc(division, 1)
                elif part == 1:
                    dve.wait_ge(division, 4 * m + 1)
                    nc.vector.scalar_tensor_tensor(den[:, side, 1], den[:, side, 0], -1.0, den[:, side, 0], ALU.mult,
                                                   ALU.max).then_inc(division, 1)
                elif part == 2:
                    dve.wait_ge(division, 4 * m + 2)
                    nc.vector.scalar_tensor_tensor(
                        den[:, side, 0], den[:, side, 1], DEN_EPS, en[:, :, at(NH * b + NH // 2 * side, NH // 2)],
                        ALU.add, ALU.max).then_inc(division, 1)
                else:
                    dve.wait_ge(division, 4 * m + 3)
                    nc.vector.reciprocal(den[:, side, 1], den[:, side, 0]).then_inc(division, 1)
                    dve.wait_ge(division, 4 * m + 4)
                    h_sb = hbuf[:, at(TPB * b, TPB)].rearrange("p t (h d) -> p t h d", h=NH)
                    nc.vector.tensor_tensor(h_sb[:, :, NH // 2 * side:NH // 2 * (side + 1)], h_ps[:, :, :, 0:DH],
                                            den[:, side, 1].unsqueeze(3).broadcast_to([P, TPB, NH // 2, DH]),
                                            ALU.mult).then_inc(h_read, 1)

            def head_stats(b, slot):
                for t in range(TPB):
                    last = nc.vector.bn_stats(h_bn[:, slot, t], hbuf[:, at(TPB * b + t)].rearrange("p o d -> p (o d)"))
                last.then_inc(h_stats, 1)

            def head_mean_var(b, slot):
                for t in range(TPB):
                    last = nc.vector.bn_aggr(h_mv[:, slot, t], h_bn[:, slot, t])
                last.then_inc(h_mv_ready, 1)

            def gain(b, slot):
                dve.wait_ge(h_mv_ready, b + 1)
                for t in range(TPB):
                    h_n = hbuf[:, at(TPB * b + t)].rearrange("p o d -> p (o d)")
                    nc.vector.scalar_tensor_tensor(h_n, h_n, h_mv[:, slot, t, 0:1], ln_gain[:], ALU.subtract,
                                                   ALU.mult).then_inc(h_gained, 1)

            def residual(b, slot, t):
                dve.wait_ge(h_gained, TPB * b + t + 1)
                if t == 0:
                    dve.wait_ge(h_rstd, b + 1)
                h_n, x_n = (a[:, at(TPB * b + t)].rearrange("p o d -> p (o d)") for a in (hbuf, xs))
                done = nc.vector.scalar_tensor_tensor(x_n, h_n, h_scale[:, slot, t:t + 1], x_n, ALU.mult, ALU.add)
                if t == TPB - 1:
                    done.then_inc(residual_added, 1)

            def residual_stats(b, t):
                done = nc.vector.bn_stats(stats[:, at(TPB * b + t)], xs[:, at(TPB * b + t)])
                if t == TPB - 1:
                    done.then_inc(x1_stats, 1)

            def mix_and_finish(b, u, i):
                for k in range(NH):
                    if k == 1 and within(b, 2, B):
                        dve.wait_ge(h_read, 2 * (b - 1))
                    if k == 1 and within(b, 3, B):
                        dve.wait_ge(residual_added, b - 2)
                    if k == 2 and within(b, 2, B):
                        dve.wait_ge(h_stats, b - 1)
                    if within(b, 0, B):
                        mix(NH // 2 * b + k // 2, k // 2 % 2, k % 2)
                    if within(b, 1, B):
                        divide(b - 1, k // 4, k % 4)
                    if within(b, 2, B):
                        if k == 1:
                            head_stats(b - 2, u)
                        if k == 2:
                            head_mean_var(b - 2, u)
                        if k == 5:
                            gain(b - 2, u)
                        if k == 7:
                            residual(b - 2, u, 0)
                        if k == 7:
                            residual(b - 2, u, 1)
                    if within(b, 3, B):
                        if k == 1:
                            residual_stats(b - 3, 0)
                        if k == 3:
                            residual_stats(b - 3, 1)

            for b in range(4):
                mix_and_finish(b, b % 2, b // 2)
            looped(dve, 2, 4, B, mix_and_finish)
            dve.wait_ge(x1_stats, B - 3)
            layer_stats(slice(0, DONE))
            for b in range(B, B + 3):
                mix_and_finish(b, b % 2, b // 2)

            def piece_low(k, slot):
                dve.wait_ge(piece_hi, k + 1)
                nc.vector.scalar_tensor_tensor(
                    w16[:, at(k), 1].rearrange("p o n -> p (o n)"), stage[:, slot], W_SCALE,
                    w16[:, at(k), 0].rearrange("p o n -> p (o n)"), ALU.mult, ALU.subtract).then_inc(piece_lo, 1)

            dve.wait_ge(x1_stats, B)
            layer_stats(slice(DONE, TT))
            dve.wait_ge(rstd_ready, 3)

            def row_low(n, u):
                dve.wait_ge(xhi_ready, n + 1)
                nc.vector.tensor_tensor(xr[:, at(n), D:2 * D].rearrange("p o d -> p (o d)"), xn[:, u % 4],
                                        xr[:, at(n), 0:D].rearrange("p o d -> p (o d)"), ALU.subtract).then_inc(xlo_ready, 1)

            def normalise(n, u, i):
                if isinstance(n, int) and n == 7:
                    dve.wait_ge(rstd_ready, 4)
                wait_from(dve, xlo_ready, n - 3)
                nc.vector.tensor_scalar(xn[:, u % 4], xs[:, at(n)].rearrange("p o d -> p (o d)"), mean[:, at(n)],
                                        rstd[:, at(n)], ALU.subtract, ALU.mult).then_inc(xn_ready, 1)
                if not isinstance(n, int) or n > 1:
                    row_low(n - 2, (u - 2) % 4)
                if isinstance(n, int) and n == 3:
                    dve.wait_ge(rg_in, 16 * C)
                    order.then(nc.vector.tensor_scalar(rg16[:, 0], rg[:], W_SCALE, None, ALU.mult))
                    nc.vector.scalar_tensor_tensor(rg16[:, 1], rg[:], W_SCALE, rg16[:, 0], ALU.mult,
                                                   ALU.subtract).then_inc(rg_ready, 1)
                if isinstance(n, int) and n in (5, 7):
                    piece_low((n - 5) // 2, (n - 5) // 2)

            stepped(dve, 8, TT, normalise)
            for n in (TT - 2, TT - 1):
                row_low(n, n % 4)
            piece_low(2, 0)

            dve.wait_ge(numbers, 1)
            dve.wait_ge(logits_done, TT)
            by_tile = lambda a: a.unsqueeze(2).broadcast_to([P, TT, E])
            by_expert = lambda a: a.unsqueeze(1).broadcast_to([P, TT, E])
            nc.vector.tensor_copy(lg[:].rearrange("p t e -> p (t e)"), ps[:, 6, 0:TT * E]).then_inc(lg_read, 1)
            dve.wait_ge(lg_read, 1)

            def pick(k, values, best):
                order.then(nc.vector.tensor_reduce(top[:, best], values[:], AX.X, ALU.max))
                order.then(nc.vector.tensor_tensor(tmp[:], values[:], by_tile(top[:, best]), ALU.is_equal))
                order.then(nc.vector.tensor_tensor(tmp[:], tmp[:], by_expert(rev[:]), ALU.mult))
                order.then(nc.vector.tensor_reduce(top[:, 2], tmp[:], AX.X, ALU.max))
                order.then(nc.vector.tensor_tensor(hot[:, k], tmp[:], by_tile(top[:, 2]), ALU.is_equal))

            pick(0, lg, 0)
            order.then(nc.vector.scalar_tensor_tensor(lg[:], hot[:, 0], -3e38, lg[:], ALU.mult, ALU.add))
            pick(1, lg, 1)
            nc.vector.tensor_tensor(hot_b[:], hot[:, 0], hot[:, 1], ALU.add).then_inc(hot_ready, 1)
            nc.vector.tensor_tensor(top[:, 3], top[:, 1], top[:, 0], ALU.subtract).then_inc(gap_ready, 1)

            def softmax_weights():
                dve.wait_ge(gap_exp, 1)
                order.then(nc.vector.tensor_scalar(top[:, 5], top[:, 4], 1.0, None, ALU.add))
                order.then(nc.vector.reciprocal(top[:, 6], top[:, 5]))
                order.then(nc.vector.tensor_scalar(top[:, 6], top[:, 6], gains[:, 1:2], None, ALU.mult))
                order.then(nc.vector.tensor_tensor(top[:, 7], top[:, 4], top[:, 6], ALU.mult))

            def expert_weights():
                order.then(nc.vector.tensor_tensor(tmp[:], hot[:, 0], by_tile(top[:, 6]), ALU.mult))
                order.then(nc.vector.tensor_tensor(pos[:], hot[:, 1], by_tile(top[:, 7]), ALU.mult))
                dve.wait_ge(meta_set, 1)
                nc.vector.tensor_tensor(meta[:, :, 0:E], tmp[:], pos[:], ALU.add).then_inc(meta_set, 1)

            def routing_ranks():
                dve.wait_ge(ranks_done, 1)
                before = ps[:, 6, 0:TT * E].rearrange("p (t e) -> p t e", e=E)
                totals = ps[:, 6, TT * E:2 * TT * E].rearrange("p (t e) -> p t e", e=E)
                for e in range(E):
                    last = nc.vector.tensor_tensor_scan(cum[:, :, e], ones_t[:], totals[:, :, e], 0.0, ALU.mult, ALU.add)
                order.then(last)
                order.then(nc.vector.tensor_tensor(pos[:], cum[:], totals, ALU.subtract))
                order.then(nc.vector.tensor_tensor(pos[:], pos[:], before, ALU.add))

            def expert_starts():
                order.then(nc.vector.tensor_tensor(fill[:], cum[:, TT - 1, :].unsqueeze(2).broadcast_to([P, E, TT]),
                                                   thresh[:].unsqueeze(1).broadcast_to([P, E, TT]), ALU.is_gt))
                order.then(nc.vector.tensor_reduce(per_e[:, 0], fill[:], AX.X, ALU.add))
                order.then(nc.vector.tensor_tensor_scan(per_e[:, 1], ones_t[:, 0:E], per_e[:, 0], 0.0, ALU.mult, ALU.add))
                order.then(nc.vector.tensor_tensor(per_e[:, 2], per_e[:, 1], per_e[:, 0], ALU.subtract))
                order.then(nc.vector.tensor_scalar(per_e[:, 3], per_e[:, 2], float(P), None, ALU.mult))
                order.then(nc.vector.tensor_tensor(pos[:], pos[:], by_expert(per_e[:, 3]), ALU.add))

            def pick_slot(k):
                order.then(nc.vector.tensor_tensor(tmp[:], pos[:], hot[:, k], ALU.mult))
                order.then(nc.vector.tensor_reduce(slot_f[:, k], tmp[:], AX.X, ALU.add))

            def both_slots():
                pick_slot(0)
                pick_slot(1)
                nc.vector.tensor_copy(slot_i[:], slot_f[:]).then_inc(routed, 1)

            def routing_tiles():
                order.then(nc.vector.tensor_tensor(past[:], count_f[:].unsqueeze(2).broadcast_to([P, NT, E]),
                                                   per_e[:, 1].unsqueeze(1).broadcast_to([P, NT, E]), ALU.is_ge))
                order.then(nc.vector.tensor_reduce(tile_f[:], past[:], AX.X, ALU.add))
                order.then(nc.vector.tensor_scalar(tile_f[:], tile_f[:], float(E - 1), None, ALU.min))
                nc.vector.tensor_copy(tile_e[:], tile_f[:]).then_inc(routed, 1)

            def routing_pads():
                order.then(nc.vector.tensor_scalar(pad_end[:, 0:E], per_e[:, 1], float(P), None, ALU.mult))
                nc.vector.tensor_tensor(pad_f[:, 0, 0:E], per_e[:, 3], cum[:, TT - 1], ALU.add)
                order.then(nc.vector.tensor_scalar(pad_f[:, 0, E:PADS], thresh[:, 0:PADS - E], pad_end[:, E - 1:E],
                                                   None, ALU.add))
                order.then(nc.vector.tensor_scalar(pad_f[:, 0], pad_f[:, 0], own_f[:, 0:1], None, ALU.add))
                order.then(nc.vector.tensor_tensor(pad_f[:, 1], pad_f[:, 0], pad_end[:], ALU.is_lt))
                order.then(nc.vector.tensor_tensor(pad_f[:, 0], pad_f[:, 0], spare_f[:], ALU.subtract))
                order.then(nc.vector.tensor_tensor(pad_f[:, 0], pad_f[:, 0], pad_f[:, 1], ALU.mult))
                order.then(nc.vector.tensor_tensor(pad_f[:, 0], pad_f[:, 0], spare_f[:], ALU.add))
                nc.vector.tensor_copy(pad_slot[:], pad_f[:, 0]).then_inc(routed, 1)

            def hid_product(n, p):
                dve.wait_ge(silu, n + 1)
                dve.wait_ge(up2, n + 1)
                wait_from(dve, hid_tr, n)
                nc.vector.tensor_tensor(hid[:], act_g[:], ps[:, 2 + p], ALU.mult).then_inc(hid_ready, 1)

            def hid_low(n, p):
                dve.wait_ge(hid_hi, n + 1)
                nc.vector.tensor_tensor(hid_t[:, 1], ps[:, 4], hid_t[:, 0], ALU.subtract).then_inc(hid_lo, 1)

            def shared_y(n, p, half):
                dve.wait_ge(down_done, n + 1)
                wait_from(dve, y_out[p], 16 * half)
                nc.vector.scalar_tensor_tensor(y[:, p], ps[:, 5, 0:D], gains[:, 1:2],
                                               xs[:, at(n)].rearrange("p o d -> p (o d)"),
                                               ALU.mult, ALU.add).then_inc(y_ready, 1)

            def shared_step(n, p, half, with_piece=True, between=None):
                hid_product(n, p)
                if not isinstance(n, int) or n > 0:
                    shared_y(n - 1, 1 - p, half if p else half - 1)
                if between:
                    between()
                hid_low(n, p)
                if with_piece:
                    piece_low(n + 2, p)

            hid_product(0, 0)
            hid_low(0, 0)
            shared_step(1, 1, 0, between=softmax_weights)
            shared_step(2, 0, 1, between=expert_weights)
            shared_step(3, 1, 1, between=routing_ranks)
            shared_step(4, 0, 2, between=expert_starts)
            shared_step(5, 1, 2, between=both_slots)
            shared_step(6, 0, 3, between=routing_tiles)
            shared_step(7, 1, 3, between=routing_pads)
            shared_step(8, 0, 4)
            looped(dve, 2, 9, PIECES - 2, shared_step)
            looped(dve, 2, PIECES - 2, TT - 1, lambda n, p, half: shared_step(n, p, half, False))
            shared_step(TT - 1, 1, (TT - 1) // 2, False)

            def expert_step(k, u, i):
                hid_product(TT + k, u % 2)
                if isinstance(k, int) and k == 0:
                    shared_y(TT - 1, 1, (TT - 1) // 2)
                hid_low(TT + k, u % 2)

            for k in range(4):
                expert_step(k, k, 0)
            looped(dve, 4, 4, NT - 3, expert_step)
            for k in range(NT - 3, NT):
                expert_step(k, k % 4, k // 4)

        @block.tensor
        def _(pe):
            pe.wait_ge(consts, 1)
            pe.wait_ge(gw_in, 32)
            for k in range(6):
                last = nc.tensor.transpose(ps[:, 5, 2 * NH * k:2 * NH * (k + 1)], gw_rows[:, P * k:P * (k + 1)],
                                           ident[0:2 * NH, 0:2 * NH])
            last.then_inc(gw_tr, 1)
            pe.wait_ge(gw_ready, 1)

            def gate_products(b, u):
                pe.wait_ge(lo_ready, 2 * b + 2)
                for t in range(TPB):
                    terms = [(w, l, c, g) for w in range(2) for c in range(C) for l, g in ((0, 0), (0, 1), (1, 0))]
                    for k, (w, l, c, g) in enumerate(terms):
                        last = nc.tensor.matmul(gates_ps[:, t, :, at(NH * b, NH)], split[:, u, w, l, c, P * t:P * (t + 1)],
                                                gw[:, w, g, c, :].rearrange("p (g h) -> p g h", g=2),
                                                start=k == 0, stop=k == len(terms) - 1)
                last.then_inc(gates_done, 1)

            def turn(b, u, i):
                p = u % 2
                wait_from(pe, lo_ready, 2 * b - 2)
                for done, src, bank in ((q_tr, qn[:, p], p), (k_tr, c_raw[:, u], 2 + p)):
                    if bank < 2:
                        pe.wait_ge(qn_ready, b + 1)
                    else:
                        pe.wait_ge(c_in[u], 16 * i + 16)
                    for t in range(TPB):
                        for c in range(C):
                            last = nc.tensor.transpose(ps[:, bank, S * c + P * t:S * c + P * (t + 1)],
                                                       src[:, t, P * c:P * (c + 1)], ident[:])
                    last.then_inc(done, 1)
                if not isinstance(b, int) or b > 0:
                    gate_products(b - 1, (u - 1) % 4)

            stepped(pe, 8, B, turn)
            gate_products(B - 1, 3)

            pe.wait_ge(g_copied, 1)
            for g in range(2):
                for t in range(TPB):
                    last = nc.tensor.transpose(ps[:, 5, S * g + P * t:S * g + P * (t + 1)], g_tok[:, t, g, :], ident[:])
            last.then_inc(g_tr, 1)
            pe.wait_ge(en_ready, 1)
            for t in range(TPB):
                last = nc.tensor.transpose(ps[:, 6, P * t:P * (t + 1)], en_h[:, P * t:P * (t + 1)], ident[:])
            last.then_inc(en_tr, 1)
            pe.wait_ge(consts, 2)
            pe.wait_ge(v_ready, B)
            pe.wait_ge(lo_ready, 2 * B)
            pe.wait_ge(am_ready, 1)
            pe.wait_ge(en_tok, 1)

            def exponents(b, u, turn, pair):
                n, q = NH // 2 * b + pair, pair % 2
                if pair == 0:
                    pe.wait_ge(heads_in[u], 8 * 16 * (turn + 1))
                wait_from(pe, decay_ready, n - 1)
                for j in range(2):
                    h = 2 * pair + j
                    bank = ps[:, 2 * q + j]
                    nc.tensor.matmul(bank[:, 0:S], a_rows[:, u, h, 0:P], m_rows[:, u, h, :], start=True, stop=False,
                                     skip_group_check=True)
                    nc.tensor.matmul(bank[:, S:S + P], a_rows[:, u, h, P:S], m_rows[:, u, h, P:S], start=False,
                                     stop=False, skip_group_check=True)
                    for k in (0, 2):
                        last = nc.tensor.matmul(bank[:, P * k:P * (k + 1)], ident_b[:], causal[:], start=False,
                                                stop=True, skip_group_check=True)
                last.then_inc(arg_ready, 1)

            def scores(b, u, pair):
                n = NH // 2 * b + pair
                for j in range(2):
                    h = 2 * pair + j
                    wait_from(pe, c_ready, 2 * n - 1 + j)
                    nc.tensor.matmul(ps[:, 4 + j, 0:S], ks[:, u, h, 0:P], qs[:, u, h, :], start=True, stop=True)
                    nc.tensor.matmul(ps[:, 4 + j, S:S + P], ks[:, u, h, P:S], qs[:, u, h, P:S], start=True,
                                     stop=True).then_inc(s_ready, 1)

            def heads(b, pair):
                n, side = NH // 2 * b + pair, pair // 2
                pe.wait_ge(c_lo, n + 1)
                if pair % 2 == 0:
                    wait_from(pe, h_read, 2 * b + side - 1)
                bank = ps[:, 6 + side, 0:TPB * (NH // 2) * (DH + 1)].rearrange("p (t h e) -> p t h e", t=TPB, h=NH // 2)
                for j in range(2):
                    h = 2 * pair + j
                    for t, blocks in ((0, ((0, 0),)), (1, ((1, 0), (2, 1)))):
                        terms = [(block, kt, a, g) for block, kt in blocks for a, g in ((0, 0), (0, 1), (1, 0))]
                        for k, (block, kt, a, g) in enumerate(terms):
                            last = nc.tensor.matmul(
                                bank[:, t, h % (NH // 2), :], c16[:, pair, a, j, P * block:P * (block + 1)],
                                v_ext[:, g, at(TPB * b + kt), h, 0:DH + 1].rearrange("p o e -> p (o e)"),
                                start=k == 0, stop=k == len(terms) - 1)
                last.then_inc(h_ready, 1)

            def attend(b, u, i, first=False, last=False):
                for pair in range(NH // 2):
                    ahead = (b, u, i, pair + 1) if pair < NH // 2 - 1 else None if last else (b + 1, 1 - u, i + u, 0)
                    if ahead:
                        exponents(*ahead)
                    if pair >= 2 or not first:
                        heads(b if pair >= 2 else b - 1, (pair - 2) % (NH // 2))
                    if ahead:
                        scores(ahead[0], ahead[1], ahead[3])

            exponents(0, 0, 0, 0)
            scores(0, 0, 0)
            attend(0, 0, 0, first=True)
            attend(1, 1, 0)
            with pe.Fori(1, B // 2 - 1) as i:
                for u in range(2):
                    attend(2 * i + u, u, i)
            attend(B - 2, 0, B // 2 - 1)
            attend(B - 1, 1, B // 2 - 1, last=True)
            for pair in (2, 3):
                heads(B - 1, pair)

            SPLIT = ((0, 0), (0, 1), (1, 0))

            def transpose_rows(bank, src):
                view = ps[:, bank, 0:D].bitcast(F16)
                for k in range(2 * C):
                    last = nc.tensor.transpose(view[:, P * k:P * (k + 1)], src[:, P * k:P * (k + 1)], ident_h[:])
                return last

            def logits(n, u):
                pe.wait_ge(row_copied, n + 1)
                terms = [(c, a, g) for c in range(C) for a, g in SPLIT]
                for k, (c, a, g) in enumerate(terms):
                    last = nc.tensor.matmul(ps[:, 6, at(E * n, E)], row_t[u][:, D * a + P * c:D * a + P * (c + 1)],
                                            rg16[:, g, c, :], start=k == 0, stop=k == len(terms) - 1)
                last.then_inc(logits_done, 1)

            def row_turn(n, u, i):
                pe.wait_ge(xlo_ready, n + 1)
                wait_from(pe, row_copied, n - 3)
                transpose_rows(u % 4, xr[:, at(n), 0:2 * D].rearrange("p o d -> p (o d)")).then_inc(row_tr, 1)
                if isinstance(n, int) and n == 2:
                    pe.wait_ge(rg_ready, 1)
                if not isinstance(n, int) or n > 1:
                    logits(n - 2, (u - 2) % 4)

            stepped(pe, 8, TT, row_turn)
            for n in (TT - 2, TT - 1):
                logits(n, n % 4)

            def ranks():
                pe.wait_ge(hot_ready, 1)
                pe.wait_ge(lg_read, 1)
                nc.tensor.matmul(ps[:, 6, 0:TT * E], earlier[:], hot_b[:].rearrange("p t e -> p (t e)"), start=True,
                                 stop=True)
                nc.tensor.matmul(ps[:, 6, TT * E:2 * TT * E], ones_b[:], hot_b[:].rearrange("p t e -> p (t e)"), start=True,
                                 stop=True).then_inc(ranks_done, 1)

            def turn_x(n, src):
                wait_from(pe, xt_ready, n)
                transpose_rows(7, src).then_inc(x_tr, 1)

            def turn_own(n):
                turn_x(n, xr[:, at(n), 0:2 * D].rearrange("p o d -> p (o d)"))

            def turn_slots(k, u, i):
                pe.wait_ge(rows_in[u], 16 * i + 16)
                turn_x(TT + k, rows[:, u, 0:2 * D])

            def up(n, p, piece):
                pe.wait_ge(xt_ready, n + 1)
                wait_from(pe, hid_ready, n - 1)
                for m, done in ((0, up1), (1, up2)):
                    terms = [(c, a, g) for c in range(C) for a, g in SPLIT]
                    for k, (c, a, g) in enumerate(terms):
                        w = w16[:, at(piece + m), g, HID * c:HID * (c + 1)].rearrange("p o n -> p (o n)")
                        last = nc.tensor.matmul(ps[:, 2 * m + p], xt[:, p, D * a + P * c:D * a + P * (c + 1)], w,
                                                start=k == 0, stop=k == len(terms) - 1)
                    last.then_inc(done, 1)

            def down(n, p, piece):
                pe.wait_ge(hid_lo, n + 1)
                terms = [(c, a, g) for c in range(KH) for a, g in SPLIT]
                for k, (c, a, g) in enumerate(terms):
                    w = w16[:, at(piece + 2), g, D * c:D * (c + 1)].rearrange("p o n -> p (o n)")
                    last = nc.tensor.matmul(ps[:, 5, 0:D], hid_t[:, a, P * c:P * (c + 1)], w,
                                            start=k == 0, stop=k == len(terms) - 1)
                last.then_inc(down_done, 1)

            def turn_hid(n, p):
                pe.wait_ge(hid_ready, n + 1)
                wait_from(pe, hid_lo, n)
                for c in range(KH):
                    last = nc.tensor.transpose(ps[:, 4, P * c:P * (c + 1)], hid[:, P * c:P * (c + 1)], ident[:])
                last.then_inc(hid_tr, 1)

            def shared_step(n, p, half):
                up(n, p, 0)
                if not isinstance(n, int) or n < TT - 1:
                    turn_own(n + 1)
                else:
                    turn_slots(0, 0, 0)
                if not isinstance(n, int) or n > 0:
                    wait_from(pe, y_ready, n - 1)
                    down(n - 1, 1 - p, 0)
                turn_hid(n, p)

            pe.wait_ge(piece_lo, 3)
            turn_own(0)
            up(0, 0, 0)
            turn_own(1)
            ranks()
            turn_hid(0, 0)
            for n in range(1, 3):
                shared_step(n, n % 2, 0)
            looped(pe, 2, 3, TT - 1, shared_step)
            shared_step(TT - 1, 1, 0)

            expert_of = [pe.alloc_register(f"expert_of{u}") for u in range(4)]

            def load_expert(k, u):
                pe.reg_load(expert_of[u], tile_e[0:1, at(k)])

            def pieces_of(u):
                return 3 + 3 * pe.snap(expert_of[u], min_val=0, max_val=E - 1)

            def expert_step(k, u, i):
                first, last = (isinstance(k, int) and k == n for n in (0, NT - 1))
                own, before = pieces_of(u), None if first else pieces_of((u - 1) % 4)
                up(TT + k, u % 2, own)
                if not last:
                    load_expert(k + 1, (u + 1) % 4)
                    turn_slots(k + 1, (u + 1) % 4, i + (u + 1) // 4)
                if first:
                    pe.wait_ge(y_ready, TT - 1)
                    down(TT - 1, 1, 0)
                else:
                    if isinstance(k, int) and k == 1:
                        pe.wait_ge(y_ready, TT)
                    else:
                        pe.wait_ge(ye_ready, k - 1)
                    down(TT + k - 1, 1 - u % 2, before)
                turn_hid(TT + k, u % 2)

            pe.wait_ge(routed, 2)
            load_expert(0, 0)
            pe.wait_ge(piece_lo, PIECES)
            for k in range(4):
                expert_step(k, k, 0)
            looped(pe, 4, 4, NT - 3, expert_step)
            for k in range(NT - 3, NT):
                expert_step(k, k % 4, k // 4)
            before = pieces_of((NT - 1) % 4)
            pe.wait_ge(ye_ready, NT - 1)
            down(TT + NT - 1, (NT - 1) % 2, before)


_INS = ['x', 'ctx_1024', 'g_xattn', 'g_ffn', 'L0_xattn_igate_w', 'L0_xattn_igate_b', 'L0_xattn_fgate_w',
        'L0_xattn_fgate_b', 'L0_xattn_ln_scale', 'L0_ffn_gate_w', 'L0_ffn_ew1', 'L0_ffn_ew2', 'L0_ffn_ew3',
        'L0_ffn_sw1', 'L0_ffn_sw2', 'L0_ffn_sw3']


def kernel(**inputs):
    import numpy as _np
    import concourse.bacc as _bacc
    from concourse import mybir as _mybir
    from concourse.bass_utils import run_bass_kernel_spmd as _run

    nc = _bacc.Bacc("TRN2", target_bir_lowering=False, num_devices=1)
    arrays, args = {}, []
    for name in _INS:
        a = _np.ascontiguousarray(inputs[name])
        arrays[f"in_{name}_dram"] = a
        args.append(nc.dram_tensor(f"in_{name}_dram", a.shape, _mybir.dt.from_np(a.dtype), kind="ExternalInput").ap())
    b, s, d = inputs['x'].shape
    args.append(nc.dram_tensor("out_0_dram", (b * s + P, d), _mybir.dt.float32, kind="ExternalOutput").ap())
    flamingo_block(nc, *args)
    r = _run(nc, [arrays], core_ids=[0])
    return r.results[0]["out_0_dram"][:b * s].reshape(b, s, d)
```
